# Optimizing a Trainium2 kernel written in Bass

```python
import numpy as np
import jax
import jax.numpy as jnp

def _softmax(x, axis=-1):
    return jax.nn.softmax(x, axis=axis)

def _gelu(x):
    return jax.nn.gelu(x, approximate=True)

def _silu(x):
    return jax.nn.silu(x)

def _sigmoid(x):
    return jax.nn.sigmoid(x)

def _layernorm(x, axis=-1, eps=1e-05):
    m = jnp.mean(x, axis=axis, keepdims=True)
    v = jnp.var(x, axis=axis, keepdims=True)
    return (x - m) / jnp.sqrt(v + eps)

def _scatter_add(tgt, idx, src, axis=0):
    return tgt.at[idx].add(src)

def _segment_sum(src, seg, n):
    return jax.ops.segment_sum(src, seg, n)
kernel_name = 'mk_xattn_ffn_d2_seqx_r4_66ac8f'

def setup_inputs(seed: int=0):
    np.random.seed(seed)
    _w = jnp.asarray

    def _rec_inputs():
        import jax
        import jax.numpy as jnp
        _rk = jax.random.key(seed)
        x = -0.0002928 + 1 * jax.random.normal(jax.random.fold_in(_rk, 1), (2, 1024, 256), jnp.float32)
        _lenS = 1024 - jax.random.randint(jax.random.fold_in(_rk, 7), (2,), 0, max(1, 1024 // 4) + 1, jnp.int32)
        _lenS2 = 64 - jax.random.randint(jax.random.fold_in(_rk, 8), (2,), 0, max(1, 64 // 4) + 1, jnp.int32)
        _ctx_1024P = jax.random.normal(jax.random.fold_in(_rk, 11), (2, 16, 256), jnp.float32)
        _ctx_1024c = jax.random.dirichlet(jax.random.fold_in(_rk, 511), 0.3 * jnp.ones((16,), jnp.float32), (2, 64))
        _ctx_1024t = jnp.einsum('bsk,bkd->bsd', _ctx_1024c, _ctx_1024P)
        _ctx_1024t = _ctx_1024t * jax.lax.rsqrt(jnp.mean(jnp.square(_ctx_1024t)) + 1e-12) * 0.953939
        ctx_1024 = -1.39393e-06 + 0.999914 * (_ctx_1024t + 0.3 * jax.random.normal(jax.random.fold_in(_rk, 611), (2, 64, 256), jnp.float32))
        return (x, ctx_1024)
    x, ctx_1024 = _rec_inputs()

    def _L0_xattn_setup():
        import jax, jax.numpy as jnp
        import numpy as np
        H = 16
        key = jax.random.key(seed)
        ks = jax.random.split(key, 7)
        B, S, D = (2, 512, 256)
        s = 1.0 / np.sqrt(D)
        return {'query': jax.random.normal(ks[0], (B, S, D), dtype=jnp.float32), 'key': jax.random.normal(ks[1], (B, S, D), dtype=jnp.float32), 'value': jax.random.normal(ks[2], (B, S, D), dtype=jnp.float32), 'W_q': jax.random.normal(ks[3], (D, D), dtype=jnp.float32) * s, 'W_k': jax.random.normal(ks[4], (D, D), dtype=jnp.float32) * s, 'W_v': jax.random.normal(ks[5], (D, D), dtype=jnp.float32) * s, 'W_fc': jax.random.normal(ks[6], (D, D), dtype=jnp.float32) * s}
    _L0_xattn_all = _L0_xattn_setup()
    _L0_xattn_in = {k: v for k, v in _L0_xattn_all.items() if k in ('W_q', 'W_k', 'W_v', 'W_fc')}
    del _L0_xattn_all

    def _L0_ffn_setup():
        import jax, jax.numpy as jnp
        import numpy as np
        HIDDEN_SIZE = 256
        NUM_EXPERTS = 8
        MOE_INTERMEDIATE_SIZE = 352
        NUM_EXPERTS_PER_TOK = 2
        SHARED_EXPERT_INTERMEDIATE_SIZE = 704
        B, T = (2, 256)
        W_SCALE = 0.02
        key = jax.random.key(seed)
        ks = jax.random.split(key, 8)
        H, E, I, SI = (HIDDEN_SIZE, NUM_EXPERTS, MOE_INTERMEDIATE_SIZE, SHARED_EXPERT_INTERMEDIATE_SIZE)
        return {'x': jax.random.normal(ks[0], (B, T, H), jnp.float32), 'gate_w': jax.random.normal(ks[1], (E, H), jnp.float32) * W_SCALE, 'experts_gate_up': jax.random.normal(ks[2], (E, 2 * I, H), jnp.float32) * W_SCALE, 'experts_down': jax.random.normal(ks[3], (E, H, I), jnp.float32) * W_SCALE, 'shared_gate_w': jax.random.normal(ks[4], (SI, H), jnp.float32) * W_SCALE, 'shared_up_w': jax.random.normal(ks[5], (SI, H), jnp.float32) * W_SCALE, 'shared_down_w': jax.random.normal(ks[6], (H, SI), jnp.float32) * W_SCALE, 'shared_expert_gate_w': jax.random.normal(ks[7], (1, H), jnp.float32) * W_SCALE}
    _L0_ffn_all = _L0_ffn_setup()
    _L0_ffn_in = {k: v for k, v in _L0_ffn_all.items() if k in ('gate_w', 'experts_gate_up', 'experts_down', 'shared_gate_w', 'shared_up_w', 'shared_down_w', 'shared_expert_gate_w')}
    del _L0_ffn_all

    def _L1_xattn_setup():
        import jax, jax.numpy as jnp
        import numpy as np
        EMBED = 256
        HEADS = 16
        HEAD_DIM = EMBED // HEADS

        def _split_heads(x):
            B, T, C = x.shape
            return x.reshape(B, T, HEADS, HEAD_DIM).transpose(0, 2, 1, 3)
        key = jax.random.key(seed)
        ks = jax.random.split(key, 11)
        B, T, C = (2, 512, EMBED)
        s = 1.0 / np.sqrt(C)
        return {'query': jax.random.normal(ks[0], (B, T, C), jnp.float32), 'key': jax.random.normal(ks[1], (B, T, C), jnp.float32), 'value': jax.random.normal(ks[2], (B, T, C), jnp.float32), 'Wq': jax.random.normal(ks[3], (C, C), jnp.float32) * s, 'bq': jnp.zeros((C,), jnp.float32), 'Wk': jax.random.normal(ks[4], (C, C), jnp.float32) * s, 'bk': jnp.zeros((C,), jnp.float32), 'Wv': jax.random.normal(ks[5], (C, C), jnp.float32) * s, 'bv': jnp.zeros((C,), jnp.float32), 'Wo': jax.random.normal(ks[6], (C, C), jnp.float32) * s, 'bo': jnp.zeros((C,), jnp.float32)}
    _L1_xattn_all = _L1_xattn_setup()
    _L1_xattn_in = {k: v for k, v in _L1_xattn_all.items() if k in ('Wq', 'bq', 'Wk', 'bk', 'Wv', 'bv', 'Wo', 'bo')}
    del _L1_xattn_all

    def _L1_ffn_setup():
        import jax, jax.numpy as jnp
        import numpy as np
        B, L, H = (8, 512, 256)
        E, K, R = (8, 2, 64)

        def _gates(cls_tok, Wr):
            logits = cls_tok @ Wr.T
            top_vals, top_idx = jax.lax.top_k(logits, K)
            neg_inf = jnp.full_like(logits, -jnp.inf)
            rows = jnp.arange(logits.shape[0])[:, None]
            masked = neg_inf.at[rows, top_idx].set(top_vals)
            return jax.nn.softmax(masked, axis=-1)
        key = jax.random.key(seed)
        k1, k2, k3, k4 = jax.random.split(key, 4)
        x = jax.random.normal(k1, (B, L, H), dtype=jnp.float32)
        Wr = jax.random.normal(k2, (E, H), dtype=jnp.float32) * (1.0 / np.sqrt(H))
        A = jax.random.normal(k3, (E, R, H), dtype=jnp.float32) * (1.0 / np.sqrt(H))
        Bw = jax.random.normal(k4, (E, H, R), dtype=jnp.float32) * (1.0 / np.sqrt(R))
        return {'x': x, 'Wr': Wr, 'A': A, 'Bw': Bw}
    _L1_ffn_all = _L1_ffn_setup()
    _L1_ffn_in = {k: v for k, v in _L1_ffn_all.items() if k in ('Wr', 'A', 'Bw')}
    del _L1_ffn_all
    return {'x': x, 'ctx_1024': ctx_1024, 'L0_xattn_W_q': _L0_xattn_in['W_q'], 'L0_xattn_W_k': _L0_xattn_in['W_k'], 'L0_xattn_W_v': _L0_xattn_in['W_v'], 'L0_xattn_W_fc': _L0_xattn_in['W_fc'], 'L0_ffn_gate_w': _L0_ffn_in['gate_w'], 'L0_ffn_experts_gate_up': _L0_ffn_in['experts_gate_up'], 'L0_ffn_experts_down': _L0_ffn_in['experts_down'], 'L0_ffn_shared_gate_w': _L0_ffn_in['shared_gate_w'], 'L0_ffn_shared_up_w': _L0_ffn_in['shared_up_w'], 'L0_ffn_shared_down_w': _L0_ffn_in['shared_down_w'], 'L0_ffn_shared_expert_gate_w': _L0_ffn_in['shared_expert_gate_w'], 'L1_xattn_Wq': _L1_xattn_in['Wq'], 'L1_xattn_bq': _L1_xattn_in['bq'], 'L1_xattn_Wk': _L1_xattn_in['Wk'], 'L1_xattn_bk': _L1_xattn_in['bk'], 'L1_xattn_Wv': _L1_xattn_in['Wv'], 'L1_xattn_bv': _L1_xattn_in['bv'], 'L1_xattn_Wo': _L1_xattn_in['Wo'], 'L1_xattn_bo': _L1_xattn_in['bo'], 'L1_ffn_Wr': _L1_ffn_in['Wr'], 'L1_ffn_A': _L1_ffn_in['A'], 'L1_ffn_Bw': _L1_ffn_in['Bw']}

def reference(x, ctx_1024, L0_xattn_W_q, L0_xattn_W_k, L0_xattn_W_v, L0_xattn_W_fc, L0_ffn_gate_w, L0_ffn_experts_gate_up, L0_ffn_experts_down, L0_ffn_shared_gate_w, L0_ffn_shared_up_w, L0_ffn_shared_down_w, L0_ffn_shared_expert_gate_w, L1_xattn_Wq, L1_xattn_bq, L1_xattn_Wk, L1_xattn_bk, L1_xattn_Wv, L1_xattn_bv, L1_xattn_Wo, L1_xattn_bo, L1_ffn_Wr, L1_ffn_A, L1_ffn_Bw):
    import jax
    import jax.numpy as jnp

    def _L0_xattn_ref(query, key, value, W_q, W_k, W_v, W_fc):
        import jax, jax.numpy as jnp
        import numpy as np
        H = 16
        B, Sq, D = query.shape
        Skv = key.shape[1]
        dh = D // H
        q = (query @ W_q.T).reshape(B, Sq, H, dh).transpose(0, 2, 1, 3)
        k = (key @ W_k.T).reshape(B, Skv, H, dh).transpose(0, 2, 1, 3)
        v = (value @ W_v.T).reshape(B, Skv, H, dh).transpose(0, 2, 1, 3)
        scores = jnp.einsum('bhqd,bhkd->bhqk', q, k) / jnp.sqrt(jnp.asarray(dh, q.dtype))
        attn = jax.nn.softmax(scores, axis=-1)
        out = jnp.einsum('bhqk,bhkd->bhqd', attn, v)
        out = out.transpose(0, 2, 1, 3).reshape(B, Sq, D)
        return out @ W_fc.T

    def _L0_ffn_ref(x, gate_w, experts_gate_up, experts_down, shared_gate_w, shared_up_w, shared_down_w, shared_expert_gate_w):
        import jax, jax.numpy as jnp
        import numpy as np
        HIDDEN_SIZE = 256
        NUM_EXPERTS = 8
        MOE_INTERMEDIATE_SIZE = 352
        NUM_EXPERTS_PER_TOK = 2
        SHARED_EXPERT_INTERMEDIATE_SIZE = 704
        B, T = (2, 256)
        W_SCALE = 0.02
        Bx, Tx, H = x.shape
        E = gate_w.shape[0]
        I = experts_down.shape[2]
        x_flat = x.reshape(Bx * Tx, H)
        logits = x_flat @ gate_w.T
        scores = jax.nn.softmax(logits, axis=-1)
        _, topk_ids = jax.lax.top_k(scores, NUM_EXPERTS_PER_TOK)
        in_topk = jax.nn.one_hot(topk_ids, E, dtype=x.dtype).sum(axis=1)
        w = scores * in_topk
        gu = jnp.einsum('nh,eih->nei', x_flat, experts_gate_up)
        g, u = (gu[..., :I], gu[..., I:])
        h = jax.nn.silu(g) * u
        expert_out = jnp.einsum('nei,ehi->neh', h, experts_down)
        out = jnp.einsum('neh,ne->nh', expert_out, w)
        shared = jax.nn.silu(x_flat @ shared_gate_w.T) * (x_flat @ shared_up_w.T) @ shared_down_w.T
        shared_weight = jax.nn.sigmoid(x_flat @ shared_expert_gate_w.T)
        out = out + shared_weight * shared
        return out.reshape(Bx, Tx, H)

    def _L1_xattn_ref(query, key, value, Wq, bq, Wk, bk, Wv, bv, Wo, bo):
        import jax, jax.numpy as jnp
        import numpy as np
        EMBED = 256
        HEADS = 16
        HEAD_DIM = EMBED // HEADS

        def _split_heads(x):
            B, T, C = x.shape
            return x.reshape(B, T, HEADS, HEAD_DIM).transpose(0, 2, 1, 3)
        scale = HEAD_DIM ** (-0.5)
        Q = _split_heads(query @ Wq + bq)
        K = _split_heads(key @ Wk + bk)
        V = _split_heads(value @ Wv + bv)
        scores = jnp.einsum('bhqd,bhkd->bhqk', Q, K) * scale
        attn = jax.nn.softmax(scores, axis=-1)
        out = jnp.einsum('bhqk,bhkd->bhqd', attn, V)
        B, H, T, D = out.shape
        out = out.transpose(0, 2, 1, 3).reshape(B, T, H * D)
        return out @ Wo + bo

    def _L1_ffn_ref(x, Wr, A, Bw):
        import jax, jax.numpy as jnp
        import numpy as np
        B, L, H = (8, 512, 256)
        E, K, R = (8, 2, 64)

        def _gates(cls_tok, Wr):
            logits = cls_tok @ Wr.T
            top_vals, top_idx = jax.lax.top_k(logits, K)
            neg_inf = jnp.full_like(logits, -jnp.inf)
            rows = jnp.arange(logits.shape[0])[:, None]
            masked = neg_inf.at[rows, top_idx].set(top_vals)
            return jax.nn.softmax(masked, axis=-1)
        gates = _gates(x[:, 0, :], Wr)
        mid = jnp.einsum('blh,erh->belr', x, A)
        expert_out = jnp.einsum('belr,ehr->belh', mid, Bw)
        weighted = jnp.einsum('be,belh->blh', gates, expert_out)
        return x + weighted
    x = x + _L0_xattn_ref(_layernorm(x, axis=-1), ctx_1024, ctx_1024, L0_xattn_W_q, L0_xattn_W_k, L0_xattn_W_v, L0_xattn_W_fc)
    x = x + _L0_ffn_ref(_layernorm(x, axis=-1), L0_ffn_gate_w, L0_ffn_experts_gate_up, L0_ffn_experts_down, L0_ffn_shared_gate_w, L0_ffn_shared_up_w, L0_ffn_shared_down_w, L0_ffn_shared_expert_gate_w)
    x = x + _L1_xattn_ref(_layernorm(x, axis=-1), ctx_1024, ctx_1024, L1_xattn_Wq, L1_xattn_bq, L1_xattn_Wk, L1_xattn_bk, L1_xattn_Wv, L1_xattn_bv, L1_xattn_Wo, L1_xattn_bo)
    x = x + _L1_ffn_ref(_layernorm(x, axis=-1), L1_ffn_Wr, L1_ffn_A, L1_ffn_Bw)
    return x

_drawn_inputs = setup_inputs


def setup_inputs(seed=0):
    import zlib

    import numpy as np

    out = dict(_drawn_inputs(seed))
    spreads = {'L1_xattn_bq': (0.0, 2.0),
     'L1_xattn_bk': (0.0, 2.0),
     'L1_xattn_bv': (0.0, 0.762),
     'L1_xattn_bo': (0.0, 0.782)}
    factors = {'L0_ffn_gate_w': 8.0,
     'L0_ffn_experts_gate_up': 8.0,
     'L0_ffn_experts_down': 8.0,
     'L0_ffn_shared_gate_w': 5.022,
     'L0_ffn_shared_up_w': 4.916,
     'L0_ffn_shared_down_w': 4.949,
     'L0_ffn_shared_expert_gate_w': 8.0}
    for name, (base, spread) in spreads.items():
        noise = np.random.default_rng([zlib.crc32(name.encode()), seed]).standard_normal(out[name].shape)
        drawn = base * np.exp(spread * noise) if base else spread * noise
        out[name] = jnp.asarray(drawn.astype(out[name].dtype))
    for name, factor in factors.items():
        out[name] = (out[name] * factor).astype(out[name].dtype)
    return out
```

```python
import concourse.bass as bass
from concourse import mybir
from contextlib import ExitStack

F32 = mybir.dt.float32
I32 = mybir.dt.int32
ALU = mybir.AluOpType
ACT = mybir.ActivationFunctionType
AX = mybir.AxisListType
ds = bass.ds

P = 128
B, S, D = 2, 1024, 256
NT = B * S // P
TB = NT // B
KD = D // P
UT = 2
UN = UT * P
NU = NT // UT
H, DH, SK = 16, 16, 64
HH = H // 2
E, I = 8, 352
KI = 3
IR = [P, P, I - 2 * P]
SI = 704
KS = 6
SR = [P] * 5 + [SI - 5 * P]
SG = 512
NB = 40
SLOTS = NB * P
R = 64
KR = E * R // P
EPS = 1e-5
SCALE = DH ** -0.5


def wait(engine, sem, value):
    if isinstance(value, int) and value <= 0:
        return
    engine.wait_ge(sem, value)


def tile0(i, b):
    return 2 * i + TB * b


def over_units(engine, unit):
    for b in range(B):
        unit(0, b, True, False)
    with engine.Fori(1, NU // 2 - 1) as i:
        for b in range(B):
            unit(i, b, False, False)
    for b in range(B):
        unit(NU // 2 - 1, b, False, True)


def over_pairs(engine, n, pair):
    pair(0)
    with engine.Fori(1, n) as i:
        pair(i)


class LayerNorm:

    def __init__(self, nc, ctx, name, mem):
        self.nc, self.mem = nc, mem
        self.stats_done = ctx.enter_context(nc.semaphore(name + "_stats_done"))
        self.mean_done = ctx.enter_context(nc.semaphore(name + "_mean_done"))
        self.var_ready = ctx.enter_context(nc.semaphore(name + "_var_ready"))
        self.rstd_ready = ctx.enter_context(nc.semaphore(name + "_rstd_ready"))
        self.xn_ready = ctx.enter_context(nc.semaphore(name + "_xn_ready"))

    def carry_wait(self, n):
        self.nc.vector.memset(self.mem["carry"][:, n:n + 1], 0.0)

    def stats(self, dve, x, i, b):
        u, m, nc = 2 * i + b, self.mem, self.nc
        for t in range(UT):
            nc.vector.bn_stats(m["stats"][:, b, t, :], x[:, ds(tile0(i, b) + t, 1), :]).then_inc(self.stats_done, 1)
        wait(dve, self.stats_done, UT * u + UT)
        self.carry_wait(0)
        for t in range(UT):
            nc.vector.bn_aggr(m["mv"][:, b, t, :], m["stats"][:, b, t, :]).then_inc(self.mean_done, 1)
        wait(dve, self.mean_done, UT * u + UT)
        nc.vector.tensor_scalar(m["var"][:, b, :], m["mv"][:, b, :, 1], EPS, None, ALU.add).then_inc(self.var_ready, 1)

    def rstd(self, pool, i, b):
        u, m, nc = 2 * i + b, self.mem, self.nc
        wait(pool, self.var_ready, u + 1)
        nc.gpsimd.tensor_tensor(m["rstd"][:, b, :], m["var"][:, b, :], m["mhalf"][:, :], ALU.pow).then_inc(self.rstd_ready, 1)

    def normalise(self, dve, x, i, b):
        u, m, nc = 2 * i + b, self.mem, self.nc
        wait(dve, self.rstd_ready, u + 1)
        for t in range(UT):
            nc.vector.tensor_scalar(m["xn"][:, b, t, :], x[:, ds(tile0(i, b) + t, 1), :].squeeze(1),
                                    m["mv"][:, b, t, 0:1], m["rstd"][:, b, t:t + 1],
                                    ALU.subtract, ALU.mult).then_inc(self.xn_ready, 1)


def kv_setup(nc, ctx, name, mem, psum, wk, wv, wsem, wcount, bk, bv, kb, vb):
    kT_ready = ctx.enter_context(nc.semaphore(name + "_kT_ready"))
    kT_sb = ctx.enter_context(nc.semaphore(name + "_kT_sb"))
    v_ready = ctx.enter_context(nc.semaphore(name + "_v_ready"))
    vb_zero = ctx.enter_context(nc.semaphore(name + "_vb_zero"))
    kv_done = ctx.enter_context(nc.semaphore(name + "_kv_done"))
    psK = psum[0][:, :].rearrange("p (h n) -> p h n", h=KD)[:, :, 0:B * SK]
    psV = psum[1][:, :].rearrange("p (b n) -> p b n", b=B)

    with nc.Block() as block:
        @block.tensor
        def _(pe):
            pe.wait_ge(wsem, wcount)
            for hf in range(KD):
                for k in range(KD):
                    last = nc.tensor.matmul(psK[:, hf, :], wk[:, k, hf * P:(hf + 1) * P], mem["ctxT"][:, k, 0, :],
                                            start=(k == 0), stop=(k == KD - 1))
            last.then_inc(kT_ready, 1)
            for b in range(B):
                for k in range(KD):
                    last = nc.tensor.matmul(psV[:, b, :], mem["ctxT"][:, k, 1 + b, :], wv[:, k, :],
                                            start=(k == 0), stop=(k == KD - 1 and bv is None))
                if bv is not None:
                    last = nc.tensor.matmul(psV[:, b, :], mem["ones_row"][0:1, :], bv[0:1, :], start=False, stop=True)
            last.then_inc(v_ready, 1)

        @block.scalar
        def _(act):
            act.wait_ge(kT_ready, 1)
            for hf in range(KD):
                if bk is None:
                    nc.scalar.activation(mem["kT"][:, hf, :], psK[:, hf, :], ACT.Copy).then_inc(kT_sb, 1)
                else:
                    nc.scalar.activation(mem["kT"][:, hf, :], psK[:, hf, :], ACT.Identity,
                                         bias=bk[:, hf:hf + 1]).then_inc(kT_sb, 1)

        @block.vector
        def _(dve):
            for b in range(B):
                nc.vector.memset(vb[b][:, :, :], 0.0).then_inc(vb_zero, 1)
            dve.wait_ge(vb_zero, B)
            dve.wait_ge(v_ready, 1)
            n = 0
            for b in range(B):
                for h2 in range(2):
                    rows = slice(h2 * SK, (h2 + 1) * SK)
                    for q in range(2):
                        at = q * 32 + h2 * DH
                        pairs = vb[b][rows, :, :].rearrange("p (g q) c -> p g q c", q=2)[:, :, q, :]
                        src = psV[rows, b, :].rearrange("p (g c) -> p g c", g=4)[:, :, at:at + DH]
                        nc.vector.tensor_copy(pairs[:, :, at:at + DH], src).then_inc(kv_done, 1)
                        nc.vector.memset(pairs[:, :, 64 + at:64 + at + DH], 1.0).then_inc(kv_done, 1)
                        n += 2
            dve.wait_ge(kT_sb, KD)
            for b in range(B):
                for hf in range(KD):
                    nc.vector.tensor_tensor(
                        kb[b][:, hf, :].rearrange("p (h k) -> p h k", h=HH),
                        mem["kT"][:, hf, b * SK:(b + 1) * SK].unsqueeze(1).to_broadcast([P, HH, SK]),
                        mem["head_of_row"][:, :].unsqueeze(2).to_broadcast([P, HH, SK]), ALU.mult).then_inc(kv_done, 1)
                    n += 1
            dve.wait_ge(kv_done, n)


def attention(nc, ctx, name, mem, psum, x, wq, wo, kb, vb, bq, bo, x_ready, x_count, combine=None):
    sem = lambda n: ctx.enter_context(nc.semaphore(f"{name}_{n}"))
    ln = LayerNorm(nc, ctx, name, mem)
    xt_ready, xT_ready, q_ready, qT_ready = sem("xt_ready"), sem("xT_ready"), sem("q_ready"), sem("qT_ready")
    s_ready, max_done, sub_done, exp_done = sem("s_ready"), sem("max_done"), sem("sub_done"), sem("exp_done")
    t_ready, pT_ready, av_ready, rc_done, o_done = sem("t_ready"), sem("pT_ready"), sem("av_ready"), sem("rc_done"), sem("o_done")
    wo_ready, resid_done, bias_done = sem("wo_ready"), sem("resid_done"), sem("bias_done")
    y1_added, y2_added, y_here = sem("y1_added"), sem("y2_added"), [sem(f"y_here{b}") for b in range(2)]
    psX = psum[0][:, :].rearrange("p (t n) -> p t n", t=2)
    psXT = psum[0][:, :].rearrange("p (k n) -> p k n", k=KD)
    psQ = psum[1][:, :].rearrange("p (k n) -> p k n", k=KD)
    psS = [psum[2], psum[3]]
    psT = [psum[4], psum[5]]
    psO = [psum[6], psum[7]]
    xn, xT, qT, p_sb, pT, oT = mem["xn"], mem["xT"], mem["qT"], mem["p"], mem["pT"], mem["oT"]
    last_u = NU - 1

    with nc.Block() as block:
        @block.tensor
        def _(pe):
            def transpose_x(i, b, first):
                u = 2 * i + b
                wait(pe, ln.xn_ready, UT * u + UT)
                wait(pe, xT_ready, u)
                wait(pe, resid_done, u - 2)
                for t in range(UT):
                    for k in range(KD):
                        last = nc.tensor.transpose(psXT[:, k, t * P:(t + 1) * P], xn[:, b, t, k * P:(k + 1) * P],
                                                   mem["ident"][:, :])
                last.then_inc(xt_ready, 1)

            def project_q(i, b):
                u = 2 * i + b
                wait(pe, xT_ready, u + 1)
                wait(pe, qT_ready, KD * u)
                for hf in range(KD):
                    for k in range(KD):
                        last = nc.tensor.matmul(psQ[:, hf, :], wq[:, k, hf * P:(hf + 1) * P], xT[:, b, k, :],
                                                start=(k == 0), stop=(k == KD - 1))
                last.then_inc(q_ready, 1)

            def scores(i, b, s):
                u = 2 * i + b
                t, hf = s // 2, s % 2
                wait(pe, qT_ready, KD * u + KD)
                wait(pe, sub_done, 4 * u + s - 1)
                nc.tensor.matmul(psS[s % 2][:, :], qT[:, b, hf, t * P:(t + 1) * P], kb[b][:, hf, :],
                                 start=True, stop=True).then_inc(s_ready, 1)

            def transpose_p(i, b, s):
                u = 2 * i + b
                wait(pe, exp_done, 4 * u + s + 1)
                wait(pe, pT_ready, 4 * u + s - 1)
                for j in range(4):
                    last = nc.tensor.transpose(psT[s % 2][:, j * P:(j + 1) * P], p_sb[:, s % 2, j * P:(j + 1) * P],
                                               mem["ident"][:, :])
                last.then_inc(t_ready, 1)

            def values(i, b, h2):
                u = 2 * i + b
                wait(pe, pT_ready, 4 * u + 4)
                wait(pe, o_done, 4 * u + 2 * h2 - 2)
                for g in (2 * h2, 2 * h2 + 1):
                    for q in range(2):
                        last = nc.tensor.matmul(psO[h2][:, (g % 2) * UN:(g % 2 + 1) * UN], vb[b][:, 2 * g + q, :],
                                                pT[:, b, 2 * g + q, :], start=(q == 0), stop=(q == 1))
                last.then_inc(av_ready, 1)

            def project_o(i, b, xT_count):
                u = 2 * i + b
                wait(pe, o_done, 4 * u + 4)
                wait(pe, xT_ready, xT_count)
                for t in range(UT):
                    for k in range(KD):
                        last = nc.tensor.matmul(psX[:, t, :], oT[:, b, k, t * P:(t + 1) * P], wo[:, k, :],
                                                start=(k == 0), stop=(k == KD - 1))
                last.then_inc(wo_ready, 1)

            def unit(i, b, first, last):
                has_prev = not (first and b == 0)
                has_next = not (last and b == 1)
                prev = (i, 0) if b else (i - 1, 1)
                nxt = (i, 1) if b == 0 else (i + 1, 0)
                scores(i, b, 0)
                scores(i, b, 1)
                if has_prev:
                    values(*prev, 0)
                transpose_p(i, b, 0)
                scores(i, b, 2)
                if has_prev:
                    values(*prev, 1)
                transpose_p(i, b, 1)
                scores(i, b, 3)
                if has_next:
                    transpose_x(*nxt, False)
                transpose_p(i, b, 2)
                if has_prev:
                    project_o(*prev, 2 * i + b + 2 if has_next else NU)
                if has_next:
                    project_q(*nxt)
                transpose_p(i, b, 3)

            transpose_x(0, 0, True)
            project_q(0, 0)
            over_units(pe, unit)
            values(NU // 2 - 1, 1, 0)
            values(NU // 2 - 1, 1, 1)
            wait(pe, resid_done, NU - 1)
            project_o(NU // 2 - 1, 1, NU)

        @block.scalar
        def _(act):
            def copy_xT(i, b):
                u = 2 * i + b
                wait(act, xt_ready, u + 1)
                wait(act, q_ready, u - 1)
                nc.scalar.activation(xT[:, b, :, :], psXT[:, :, :], ACT.Copy).then_inc(xT_ready, 1)

            def copy_q(i, b):
                u = 2 * i + b
                wait(act, q_ready, u + 1)
                wait(act, s_ready, 4 * u - 4)
                for hf in range(KD):
                    if bq is None:
                        nc.scalar.activation(qT[:, b, hf, :], psQ[:, hf, :], ACT.Copy).then_inc(qT_ready, 1)
                    else:
                        nc.scalar.activation(qT[:, b, hf, :], psQ[:, hf, :], ACT.Identity,
                                             bias=bq[:, hf:hf + 1]).then_inc(qT_ready, 1)

            def exps(i, b, s):
                u = 2 * i + b
                wait(act, sub_done, 4 * u + s + 1)
                wait(act, t_ready, 4 * u + s - 1)
                nc.scalar.activation(p_sb[:, s % 2, :], mem["sx"][:, s % 2, :], ACT.Exp, scale=SCALE).then_inc(exp_done, 1)

            def copy_pT(i, b, s):
                u = 2 * i + b
                t, hf = s // 2, s % 2
                wait(act, t_ready, 4 * u + s + 1)
                wait(act, av_ready, 2 * u - 2)
                nc.scalar.activation(pT[:, b, hf * 4:(hf + 1) * 4, t * P:(t + 1) * P],
                                     psT[s % 2][:, :].rearrange("p (j n) -> p j n", j=4), ACT.Copy).then_inc(pT_ready, 1)

            def unit(i, b, first, last):
                has_next = not (last and b == 1)
                nxt = (i, 1) if b == 0 else (i + 1, 0)
                exps(i, b, 0)
                exps(i, b, 1)
                copy_pT(i, b, 0)
                exps(i, b, 2)
                copy_pT(i, b, 1)
                if has_next:
                    copy_xT(*nxt)
                exps(i, b, 3)
                copy_pT(i, b, 2)
                if has_next:
                    copy_q(*nxt)
                copy_pT(i, b, 3)

            copy_xT(0, 0)
            copy_q(0, 0)
            over_units(act, unit)

        @block.vector
        def _(dve):
            def softmax_shift(i, b, s):
                u = 2 * i + b
                sc = psS[s % 2][:, :].rearrange("p (h k) -> p h k", h=HH)
                mx = mem["mx"][:, s % 2, :]
                wait(dve, s_ready, 4 * u + s + 1)
                nc.vector.tensor_reduce(mx, sc, AX.X, ALU.max).then_inc(max_done, 1)
                wait(dve, max_done, 4 * u + s + 1)
                wait(dve, exp_done, 4 * u + s - 1)
                nc.vector.tensor_tensor(mem["sx"][:, s % 2, :].rearrange("p (h k) -> p h k", h=HH), sc,
                                        mx.unsqueeze(2).to_broadcast([P, HH, SK]), ALU.subtract).then_inc(sub_done, 1)

            def divide(i, b, h2):
                u = 2 * i + b
                wait(dve, av_ready, 2 * u + h2 + 1)
                nc.vector.reciprocal(mem["rc"][:, h2, :], psO[h2][64:128, :]).then_inc(rc_done, 1)
                wait(dve, rc_done, 2 * u + h2 + 1)
                wait(dve, wo_ready, u - 1)
                for g in range(2):
                    nc.vector.tensor_tensor(oT[g * 64:(g + 1) * 64, b, h2, :], psO[h2][0:64, g * UN:(g + 1) * UN],
                                            mem["rc"][:, h2, g * UN:(g + 1) * UN], ALU.mult).then_inc(o_done, 1)

            def residual(i, b):
                u = 2 * i + b
                wait(dve, wo_ready, u + 1)
                if bo is not None:
                    wait(dve, bias_done, UT * u + UT)
                rows = x[:, ds(tile0(i, b), UT), :]
                nc.vector.tensor_tensor(rows, psX[:, :, :], rows, ALU.add).then_inc(resid_done, 1)

            def norm_first(i, b):
                u = 2 * i + b
                if combine is not None:
                    wait(dve, y_here[b], 64 * i + 64)
                    for j in range(2):
                        for t in range(UT):
                            rows = x[:, ds(tile0(i, b) + t, 1), :].squeeze(1)
                            nc.vector.scalar_tensor_tensor(rows, mem["yg"][:, b, t, j, :],
                                                           combine["w"][:, j, ds(tile0(i, b) + t, 1)], rows,
                                                           ALU.mult, ALU.add).then_inc((y1_added, y2_added)[j], 1)
                        wait(dve, (y1_added, y2_added)[j], UT * u + UT)
                    ln.carry_wait(1)
                ln.stats(dve, x, i, b)

            def norm_second(i, b):
                wait(dve, xt_ready, 2 * i + b - 1)
                ln.normalise(dve, x, i, b)

            def unit(i, b, first, last):
                has_prev = not (first and b == 0)
                has_next = not (last and b == 1)
                prev = (i, 0) if b else (i - 1, 1)
                nxt = (i, 1) if b == 0 else (i + 1, 0)
                softmax_shift(i, b, 0)
                softmax_shift(i, b, 1)
                if has_next:
                    norm_first(*nxt)
                if has_prev:
                    divide(*prev, 0)
                softmax_shift(i, b, 2)
                if has_next:
                    norm_second(*nxt)
                if has_prev:
                    divide(*prev, 1)
                softmax_shift(i, b, 3)
                if has_prev:
                    residual(*prev)

            wait(dve, x_ready, x_count)
            norm_first(0, 0)
            norm_second(0, 0)
            over_units(dve, unit)
            for h2 in range(2):
                divide(NU // 2 - 1, 1, h2)
            residual(NU // 2 - 1, 1)
            dve.wait_ge(resid_done, NU)

        @block.gpsimd
        def _(pool):
            def gather(i, b):
                u = 2 * i + b
                wait(pool, y2_added, UT * (u - 1))
                for t in range(UT):
                    for j in range(2):
                        tl = tile0(i, b) + t
                        pool.indirect_dma_start(mem["yg"][:, b, t, j, :], None, combine["y"][:, :],
                                                bass.IndirectOffsetOnAxis(ap=combine["slot"][:, j, tl:tl + 1], axis=0),
                                                bounds_check=SLOTS - 1).then_inc(y_here[b], 16)

            def unit(i, b, *_):
                ln.rstd(pool, i, b)
                if bo is not None:
                    wait(pool, ln.xn_ready, UT * (2 * i + b) + UT)
                    for t in range(UT):
                        rows = x[:, ds(tile0(i, b) + t, 1), :].squeeze(1)
                        nc.gpsimd.tensor_tensor(rows, rows, bo[:, :], ALU.add).then_inc(bias_done, 1)

            if combine is None:
                over_units(pool, unit)
            else:
                gather(0, 0)
                gather(0, 1)
                for i in range(NU // 2):
                    for b in range(B):
                        unit(i, b)
                        if i + 1 < NU // 2:
                            gather(i + 1, b)


def top_two(nc, dve, sem, base, p, rev, work, shape, low):
    key, top1, hot1, rest, top2, hot2, kmax = work
    n = base

    def link(ins):
        nonlocal n
        n += 1
        ins.then_inc(sem, 1)
        dve.wait_ge(sem, n)

    wide = lambda a: a.unsqueeze(len(shape) - 1).to_broadcast(shape)
    v = nc.vector
    for src, top, hot in ((p, top1, hot1), (rest, top2, hot2)):
        link(v.tensor_reduce(top, src, AX.X, ALU.max))
        link(v.tensor_tensor(key, src, wide(top), ALU.is_equal))
        link(v.tensor_tensor(key, key, rev, ALU.mult))
        link(v.tensor_reduce(kmax, key, AX.X, ALU.max))
        link(v.tensor_tensor(hot, key, wide(kmax), ALU.is_equal))
        if src is p:
            link(v.scalar_tensor_tensor(rest, hot, low, p, ALU.mult, ALU.add))
    return n


def xattn_ffn_kernel(nc, x_in, ctxT_in, wq0, wk0, wv0, wo0, gate_in, egu_in, edown_in, sgate_in, sup_in, sdown_in,
                     wq1, bq1, wk1, bk1, wv1, bv1, wo1, bo1, wr_in, a_in, bw_in, out):
    ctx = ExitStack()
    with ctx:
        def sb(name, shape, dt=F32):
            return ctx.enter_context(nc.sbuf_tensor(name, shape, dt))

        def sem(name):
            return ctx.enter_context(nc.semaphore(name))

        psum = [ctx.enter_context(nc.psum_tensor(f"bank{n}", [P, 512], F32)) for n in range(8)]
        xg_dram = nc.dram_tensor("expert_rows_in", [SLOTS, D], F32, kind="Internal").ap()
        yg_dram = nc.dram_tensor("expert_rows_out", [SLOTS, D], F32, kind="Internal").ap()

        x = sb("x", [P, NT, D])
        xn2 = sb("xn2", [P, NT, D])
        mem = {
            "ident": sb("ident", [P, P]), "ones_row": sb("ones_row", [1, P]),
            "head_of_row": sb("head_of_row", [P, HH]), "ctxT": sb("ctxT", [P, KD, 1 + B, P]),
            "kT": sb("kT", [P, KD, B * SK]),
            "stats": sb("stats", [P, 2, UT, 6]), "mv": sb("mv", [P, 2, UT, 2]), "var": sb("var", [P, 2, UT]),
            "rstd": sb("rstd", [P, 2, UT]), "carry": sb("carry", [P, 2]), "mhalf": sb("mhalf", [P, UT]),
            "xn": sb("xn", [P, 2, UT, D]), "xT": sb("xT", [P, 2, KD, UN]), "qT": sb("qT", [P, 2, KD, UN]),
            "mx": sb("mx", [P, 2, HH]), "sx": sb("sx", [P, 2, 512]), "p": sb("p", [P, 2, 512]),
            "rc": sb("rc", [64, 2, 512]),
        }
        big = sb("big", [P, 13 * 512])
        mem["pT"] = xn2[:, :, :].rearrange("p (b j) n -> p b j n", b=2)
        mem["oT"] = big[:, 0:1024].rearrange("p (b k n) -> p b k n", b=2, k=KD)
        mem["yg"] = big[:, 1024:3072].rearrange("p (b t j n) -> p b t j n", b=2, t=UT, j=2)
        wq = [sb("wq", [P, KD, D])] * 2
        wo = [sb("wo", [P, KD, D])] * 2
        wk = sb("wk", [P, KD, D])
        wv = sb("wv", [P, KD, D])
        kvb = sb("kvb", [P, 8 * 512])
        kb = [kvb[:, b * 1024:(b + 1) * 1024].rearrange("p (h n) -> p h n", h=KD) for b in range(B)]
        vb = [kvb[:, (2 + b) * 1024:(3 + b) * 1024].rearrange("p (j n) -> p j n", j=8) for b in range(B)]
        bcol = sb("bcol", [P, 2, KD])
        bvrow = sb("bvrow", [1, D])
        bo_all = sb("bo_all", [P, D])
        gw = sb("gw", [P, KD, E + 1])
        egu = sb("egu", [P, KD, E * 2 * I])
        edn = sb("edn", [P, KI, E * D])
        sgu = sb("sgu", [P, 2, KD, SI])
        sdn = sb("sdn", [P, KS, D])

        x_in_done, attn0_in, attn1_in, router_in, shared_in, expert_in, ffn1_in = (
            sem("x_in_done"), sem("attn0_in"), sem("attn1_in"), sem("router_in"), sem("shared_in"), sem("expert_in"), sem("ffn1_in"))
        made, zero_made, rows_zeroed = sem("made"), sem("zero_made"), sem("rows_zeroed")
        split = lambda a: a.rearrange("(k p) n -> p k n", p=P)
        with nc.Block() as block:
            @block.sync
            def _(sp):
                sp.dma_start(mem["ctxT"][:, :, 0, :], split(ctxT_in)).then_inc(attn0_in, 16)
                for b in range(B):
                    for c in range(2):
                        sp.dma_start(mem["ctxT"][:, :, 1 + b, c * SK:(c + 1) * SK],
                                     split(ctxT_in)[:, :, b * SK:(b + 1) * SK]).then_inc(attn0_in, 16)
                sp.dma_start(wk[:, :, :], split(wk0)).then_inc(attn0_in, 16)
                sp.dma_start(wv[:, :, :], split(wv0)).then_inc(attn0_in, 16)
                sp.dma_start(wq[0][:, :, :], split(wq0)).then_inc(attn0_in, 16)
                sp.dma_start(wo[0][:, :, :], split(wo0)).then_inc(attn0_in, 16)
                sp.dma_start(gw[:, :, :], split(gate_in)).then_inc(router_in, 16)
                sp.dma_start(sgu[:, 0, :, :], split(sgate_in)).then_inc(shared_in, 16)
                sp.dma_start(sgu[:, 1, :, :], split(sup_in)).then_inc(shared_in, 16)
                sp.dma_start(sdn[:, 0:5, :], split(sdown_in[0:5 * P, :])).then_inc(shared_in, 16)
                sp.dma_start(sdn[0:SR[5], 5, :], sdown_in[5 * P:SI, :]).then_inc(shared_in, 16)
                sp.wait_ge(zero_made, 1)
                sp.dma_start(xg_dram.rearrange("(c p) d -> p c d", p=P), 
                             big[:, 0:D].unsqueeze(1).to_broadcast([P, NB, D])).then_inc(rows_zeroed, 16)
                sp.wait_ge(rows_zeroed, 16)

            @block.scalar
            def _(act):
                for c in range(4):
                    act.dma_start(x[:, 4 * c:4 * c + 4, :],
                                  x_in[4 * c * P:(4 * c + 4) * P, :].rearrange("(t p) n -> p t n", p=P)).then_inc(x_in_done, 16)
                act.dma_start(egu[:, :, :], split(egu_in)).then_inc(expert_in, 16)
                act.dma_start(edn[:, 0:2, :], split(edown_in[0:2 * P, :])).then_inc(expert_in, 16)
                act.dma_start(edn[0:IR[2], 2, :], edown_in[2 * P:I, :]).then_inc(expert_in, 16)

            @block.vector
            def _(dve):
                nc.vector.memset(big[:, 0:D], 0.0).then_inc(zero_made, 1)
                nc.vector.memset(mem["ones_row"][:, :], 1.0).then_inc(made, 1)
                nc.vector.memset(mem["mhalf"][:, :], -0.5).then_inc(made, 1)

            @block.gpsimd
            def _(pool):
                nc.gpsimd.memset(mem["ident"][:, :], 0.0).then_inc(made, 1)
                nc.gpsimd.memset(mem["head_of_row"][:, :], 1.0).then_inc(made, 1)
                pool.wait_ge(made, 4)
                nc.gpsimd.affine_select(out=mem["ident"][:, :], in_=mem["ident"][:, :], compare_op=ALU.not_equal, fill=1.0,
                                        base=0, pattern=[[-1, P]], channel_multiplier=1).then_inc(made, 1)
                nc.gpsimd.affine_select(out=mem["head_of_row"][:, :], in_=mem["head_of_row"][:, :], compare_op=ALU.is_ge,
                                        fill=0.0, base=0, pattern=[[-DH, HH]], channel_multiplier=1).then_inc(made, 1)
                pool.wait_ge(made, 6)
                nc.gpsimd.affine_select(out=mem["head_of_row"][:, :], in_=mem["head_of_row"][:, :], compare_op=ALU.is_ge,
                                        fill=0.0, base=DH - 1, pattern=[[DH, HH]], channel_multiplier=-1).then_inc(made, 1)
                pool.wait_ge(made, 7)

        kv_setup(nc, ctx, "kv0", mem, psum, wk, wv, attn0_in, 16 * 9, None, None, kb, vb)
        attention(nc, ctx, "attn0", mem, psum, x, wq[0], wo[0], kb, vb, None, None, x_in_done, 64)

        xn2T = kvb[:, :].rearrange("p (k n) -> p k n", k=KD)
        lg = sb("lg", [P, NT, E + 1])
        ln = LayerNorm(nc, ctx, "ln2", mem)
        xt_ready, xT_ready, xT2_ready, kept, lg_ready, lg_taken = (
            sem("r_xt_ready"), sem("r_xT_ready"), sem("r_xT2_ready"), sem("r_kept"), sem("r_lg_ready"), sem("r_lg_taken"))
        xTv = mem["xT"]
        with nc.Block() as block:
            @block.sync
            def _(sp):
                for dst, src in ((wk, wk1), (wv, wv1), (wq[1], wq1), (wo[1], wo1)):
                    sp.dma_start(dst[:, :, :], split(src)).then_inc(attn1_in, 16)
                for n, src in enumerate((bq1, bk1)):
                    sp.dma_start(bcol[:, n, :], src.rearrange("(k p) -> p k", p=P),
                                 allow_slow_non_contiguous=True).then_inc(attn1_in, 16)
                sp.dma_start(bvrow[:, :], bv1.rearrange("(a n) -> a n", a=1)).then_inc(attn1_in, 16)
                sp.dma_start(bo_all[:, :], bo1.partition_broadcast(P)).then_inc(attn1_in, 16)

            @block.vector
            def _(dve):
                def keep_xT(i, b):
                    u = 2 * i + b
                    wait(dve, xt_ready, u + 1)
                    for k in range(KD):
                        nc.vector.tensor_copy(xn2T[:, k, ds(tile0(i, b) * P, UN)], psum[b][:, k * UN:(k + 1) * UN]).then_inc(xT2_ready, 1)

                def keep_logits(i, b):
                    wait(dve, lg_ready, 2 * i + b + 1)
                    nc.vector.tensor_copy(lg[:, ds(tile0(i, b), UT), :],
                                          psum[2 + b][:, 0:UT * (E + 1)].rearrange("p (t e) -> p t e", t=UT)).then_inc(lg_taken, 1)

                def unit(i, b, first, last):
                    ln.stats(dve, x, i, b)
                    prev = (i, 0) if b else (i - 1, 1)
                    if not (first and b == 0):
                        keep_xT(*prev)
                    wait(dve, kept, UT * (2 * i + b - 1))
                    wait(dve, xt_ready, 2 * i + b - 1)
                    ln.normalise(dve, x, i, b)
                    if not (first and b == 0):
                        keep_logits(*prev)

                over_units(dve, unit)
                keep_xT(NU // 2 - 1, 1)
                keep_logits(NU // 2 - 1, 1)
                dve.wait_ge(lg_taken, NU)

            @block.gpsimd
            def _(pool):
                def unit(i, b, *_):
                    ln.rstd(pool, i, b)
                    wait(pool, ln.xn_ready, UT * (2 * i + b) + UT)
                    for t in range(UT):
                        nc.gpsimd.tensor_copy(xn2[:, ds(tile0(i, b) + t, 1), :], mem["xn"][:, b, t:t + 1, :]).then_inc(kept, 1)
                over_units(pool, unit)

            @block.tensor
            def _(pe):
                pe.wait_ge(router_in, 16)

                def route(i, b):
                    u = 2 * i + b
                    wait(pe, xT_ready, u + 1)
                    wait(pe, lg_taken, u - 1)
                    for t in range(UT):
                        for k in range(KD):
                            last = nc.tensor.matmul(psum[2 + b][:, t * (E + 1):(t + 1) * (E + 1)],
                                                    xTv[:, b, k, t * P:(t + 1) * P], gw[:, k, :],
                                                    start=(k == 0), stop=(k == KD - 1))
                    last.then_inc(lg_ready, 1)

                def unit(i, b, first, last_pair):
                    u = 2 * i + b
                    wait(pe, ln.xn_ready, UT * u + UT)
                    wait(pe, xT_ready, u - 1)
                    wait(pe, xT2_ready, KD * (u - 1))
                    for t in range(UT):
                        for k in range(KD):
                            last = nc.tensor.transpose(psum[b][:, k * UN + t * P:k * UN + (t + 1) * P],
                                                       mem["xn"][:, b, t, k * P:(k + 1) * P], mem["ident"][:, :])
                    last.then_inc(xt_ready, 1)
                    if not (first and b == 0):
                        route(*((i, 0) if b else (i - 1, 1)))

                over_units(pe, unit)
                route(NU // 2 - 1, 1)

            @block.scalar
            def _(act):
                def unit(i, b, *_):
                    u = 2 * i + b
                    wait(act, xt_ready, u + 1)
                    wait(act, xT2_ready, KD * (u + 1))
                    wait(act, lg_ready, u - 1)
                    nc.scalar.activation(xTv[:, b, :, :], psum[b][:, :].rearrange("p (k n) -> p k n", k=KD),
                                         ACT.Copy).then_inc(xT_ready, 1)
                over_units(act, unit)

        hot = {n: sb("rt_" + n, [P, NT, E]) for n in ("p", "key", "hot1", "rest", "hot2", "mask", "slots")}
        col = {n: sb("rc_" + n, [P, NT]) for n in ("max", "sum", "inv", "kmax", "sg")}
        wtop = sb("wtop", [P, 2, NT])
        slot_f = sb("slot_f", [P, 2, NT])
        slot = sb("slot", [P, 2, NT], I32)
        rev = sb("rev", [P, E])
        before = sb("before", [P, P])
        ones = sb("ones", [P, P])
        thr = sb("thr", [P, NT])
        blk = sb("blk", [P, NB])
        cnt = sb("cnt", [P, 4, E])
        cmp_n = sb("cmp_n", [P, E, NT])
        cmp_b = sb("cmp_b", [P, NB, E])
        be_f = sb("be_f", [P, NB])
        be = sb("be", [1, NB], I32)
        one8 = sb("one8", [P, E])
        cst, rt, ex_done, masked, ranked, routed, scattered = (
            sem("cst"), sem("rt"), sem("ex_done"), sem("masked"), sem("ranked"), sem("routed"), sem("scattered"))
        g_ready, u_ready, silu_done, h_done, d_ready, sh_added = (
            sem("sh_g_ready"), sem("sh_u_ready"), sem("sh_silu_done"), sem("sh_h_done"), sem("sh_d_ready"), sem("sh_added"))
        act_s = mem["sx"]
        hT = big[:, 0:2 * KS * SG].rearrange("p (b j n) -> p b j n", b=2, j=KS)
        NSG = NT * P // SG
        with nc.Block() as block:
            @block.gpsimd
            def _(pool):
                nc.gpsimd.iota(rev[:, :], [[-1, E]], base=E, channel_multiplier=0, allow_small_or_imprecise_dtypes=True).then_inc(cst, 1)
                nc.gpsimd.iota(thr[:, :], [[P, NT]], base=0, channel_multiplier=0, allow_small_or_imprecise_dtypes=True).then_inc(cst, 1)
                nc.gpsimd.iota(blk[:, :], [[1, NB]], base=0, channel_multiplier=0, allow_small_or_imprecise_dtypes=True).then_inc(cst, 1)
                nc.gpsimd.memset(ones[:, :], 1.0).then_inc(cst, 1)
                nc.gpsimd.memset(before[:, :], 1.0).then_inc(cst, 1)
                nc.gpsimd.memset(one8[:, :], 1.0).then_inc(cst, 1)
                pool.wait_ge(cst, 6)
                nc.gpsimd.affine_select(out=before[:, :], in_=before[:, :], compare_op=ALU.is_ge, fill=0.0,
                                        base=-1, pattern=[[1, P]], channel_multiplier=-1).then_inc(cst, 1)
                pool.wait_ge(routed, 1)
                for t in range(NT):
                    for j in range(2):
                        pool.indirect_dma_start(xg_dram[:, :], bass.IndirectOffsetOnAxis(ap=slot[:, j, t:t + 1], axis=0),
                                                xn2[:, t, :], None, bounds_check=SLOTS - 1).then_inc(scattered, 16)
                pool.wait_ge(scattered, 16 * 2 * NT)

            @block.scalar
            def _(act):
                act.wait_ge(rt, 2)
                nc.scalar.activation(hot["p"][:, :, :], hot["p"][:, :, :], ACT.Exp).then_inc(ex_done, 1)
                nc.scalar.activation(col["sg"][:, :], lg[:, :, E], ACT.Exp, scale=-1.0).then_inc(ex_done, 1)

                def group(gi, par, first):
                    for j in range(KS):
                        n = KS * (2 * gi + par) + j
                        rows = SR[j]
                        wait(act, g_ready, n + 1)
                        wait(act, h_done, n - 1)
                        nc.scalar.activation(act_s[0:rows, j % 2, :], psum[j % 2][0:rows, :], ACT.Silu).then_inc(silu_done, 1)
                over_pairs(act, NSG // 2, lambda gi: [group(gi, par, False) for par in range(2)])

            @block.tensor
            def _(pe):
                rank = psum[6][:, 0:(NT + 1) * E].rearrange("p (t e) -> p t e", e=E)
                pe.wait_ge(masked, 1)
                pe.wait_ge(cst, 7)
                for t in range(NT):
                    nc.tensor.matmul(rank[:, t + 1:NT + 1, :], ones[:, :],
                                     hot["mask"][:, t:t + 1, :].to_broadcast([P, NT - t, E]),
                                     start=(t == 0), stop=False, skip_group_check=True)
                nc.tensor.matmul(rank[:, 0:1, :], before[:, :], hot["mask"][:, 0:1, :], start=False, stop=False,
                                 skip_group_check=True)
                nc.tensor.matmul(rank[:, 1:NT, :], before[:, :], hot["mask"][:, 1:NT, :], start=False, stop=True,
                                 skip_group_check=True).then_inc(ranked, 1)
                pe.wait_ge(shared_in, 64)

                def up(gi, par):
                    for j in range(KS):
                        n = KS * (2 * gi + par) + j
                        rows = SR[j]
                        wait(pe, silu_done, n - 1)
                        wait(pe, h_done, n - 1)
                        for w, bank, done in ((0, j % 2, g_ready), (1, 2 + j % 2, u_ready)):
                            for k in range(KD):
                                last = nc.tensor.matmul(psum[bank][0:rows, :], sgu[:, w, k, j * P:j * P + rows],
                                                        xn2T[:, k, ds((2 * gi + par) * SG, SG)],
                                                        start=(k == 0), stop=(k == KD - 1))
                            last.then_inc(done, 1)

                def down(gi, par):
                    g = 2 * gi + par
                    wait(pe, h_done, KS * g + KS)
                    for c in range(2):
                        wait(pe, sh_added, 4 * g + 2 * c - 2)
                        for t in range(2):
                            for j in range(KS):
                                last = nc.tensor.matmul(psum[4 + c][:, t * D:(t + 1) * D],
                                                        hT[0:SR[j], par, j, (2 * c + t) * P:(2 * c + t + 1) * P],
                                                        sdn[0:SR[j], j, :], start=(j == 0), stop=(j == KS - 1))
                            last.then_inc(d_ready, 1)

                def pair(gi):
                    up(gi, 0)
                    up(gi, 1)
                    down(gi, 0)
                    down(gi, 1)

                over_pairs(pe, NSG // 2, pair)

            @block.vector
            def _(dve):
                v = nc.vector
                n = 0

                def link(ins):
                    nonlocal n
                    n += 1
                    ins.then_inc(rt, 1)
                    dve.wait_ge(rt, n)

                wide = lambda a: a.unsqueeze(2).to_broadcast([P, NT, E])
                link(v.tensor_reduce(col["max"][:, :], lg[:, :, 0:E], AX.X, ALU.max))
                link(v.tensor_tensor(hot["p"][:, :, :], lg[:, :, 0:E], wide(col["max"][:, :]), ALU.subtract))
                dve.wait_ge(ex_done, 2)
                link(v.tensor_reduce(col["sum"][:, :], hot["p"][:, :, :], AX.X, ALU.add))
                link(v.reciprocal(col["inv"][:, :], col["sum"][:, :]))
                link(v.tensor_tensor(hot["p"][:, :, :], hot["p"][:, :, :], wide(col["inv"][:, :]), ALU.mult))
                link(v.tensor_scalar(col["sg"][:, :], col["sg"][:, :], 1.0, None, ALU.add))
                link(v.reciprocal(col["sg"][:, :], col["sg"][:, :]))
                dve.wait_ge(cst, 7)
                n = top_two(nc, dve, rt, n, hot["p"][:, :, :], rev[:, :].unsqueeze(1).to_broadcast([P, NT, E]),
                            (hot["key"][:, :, :], wtop[:, 0, :], hot["hot1"][:, :, :], hot["rest"][:, :, :],
                             wtop[:, 1, :], hot["hot2"][:, :, :], col["kmax"][:, :]), [P, NT, E], -2.0)
                v.tensor_tensor(hot["mask"][:, :, :], hot["hot1"][:, :, :], hot["hot2"][:, :, :], ALU.add).then_inc(masked, 1)
                dve.wait_ge(ranked, 1)
                rank = psum[6][:, 0:(NT + 1) * E].rearrange("p (t e) -> p t e", e=E)
                link(v.tensor_copy(cnt[:, 0, :], rank[:, NT, :]))
                link(v.tensor_tensor(cmp_n[:, :, :], cnt[:, 0, :].unsqueeze(2).to_broadcast([P, E, NT]),
                                     thr[:, :].unsqueeze(1).to_broadcast([P, E, NT]), ALU.is_gt))
                link(v.tensor_reduce(cnt[:, 1, :], cmp_n[:, :, :], AX.X, ALU.add))
                link(v.tensor_tensor_scan(cnt[:, 2, :], one8[:, :], cnt[:, 1, :], 0.0, ALU.mult, ALU.add))
                link(v.tensor_tensor(cnt[:, 3, :], cnt[:, 2, :], cnt[:, 1, :], ALU.subtract))
                link(v.tensor_scalar(cnt[:, 3, :], cnt[:, 3, :], float(P), None, ALU.mult))
                link(v.tensor_tensor(hot["slots"][:, :, :], rank[:, 0:NT, :],
                                     cnt[:, 3, :].unsqueeze(1).to_broadcast([P, NT, E]), ALU.add))
                for j, h in enumerate(("hot1", "hot2")):
                    link(v.tensor_tensor(hot["key"][:, :, :], hot[h][:, :, :], hot["slots"][:, :, :], ALU.mult))
                    link(v.tensor_reduce(slot_f[:, j, :], hot["key"][:, :, :], AX.X, ALU.add))
                link(v.tensor_tensor(cmp_b[:, :, :], cnt[:, 2, :].unsqueeze(1).to_broadcast([P, NB, E]),
                                     blk[:, :].unsqueeze(2).to_broadcast([P, NB, E]), ALU.is_le))
                link(v.tensor_reduce(be_f[:, :], cmp_b[:, :, :], AX.X, ALU.add))
                link(v.tensor_scalar(be_f[:, :], be_f[:, :], float(E - 1), None, ALU.min))
                link(v.tensor_copy(be[:, :], be_f[0:1, :]))
                v.tensor_copy(slot[:, :, :], slot_f[:, :, :]).then_inc(routed, 1)

                def hidden(gi, par):
                    for j in range(KS):
                        n = KS * (2 * gi + par) + j
                        rows = SR[j]
                        wait(dve, silu_done, n + 1)
                        wait(dve, u_ready, n + 1)
                        wait(dve, d_ready, 4 * (2 * gi + par - 1))
                        v.tensor_tensor(hT[0:rows, par, j, :], psum[2 + j % 2][0:rows, :], act_s[0:rows, j % 2, :],
                                        ALU.mult).then_inc(h_done, 1)

                def add(gi, par):
                    g = 2 * gi + par
                    for t in range(4):
                        wait(dve, d_ready, 4 * g + 2 * (t // 2) + 2)
                        rows = x[:, ds(4 * g + t, 1), :].squeeze(1)
                        v.scalar_tensor_tensor(rows, psum[4 + t // 2][:, (t % 2) * D:(t % 2 + 1) * D],
                                               col["sg"][:, ds(4 * g + t, 1)], rows, ALU.mult, ALU.add).then_inc(sh_added, 1)

                def pair(gi):
                    hidden(gi, 0)
                    hidden(gi, 1)
                    add(gi, 0)
                    add(gi, 1)

                over_pairs(dve, NSG // 2, pair)
                dve.wait_ge(sh_added, NT)

        at, parts = 0, {}
        for name, shape in (("xg", (2, D)), ("xgT", (2, KD * P)), ("hh", (2, I)), ("hg", (2, I)), ("hgT", (2, KI * P)),
                            ("yy", (2, D))):
            parts[name] = big[:, at:at + shape[0] * shape[1]].rearrange("p (c n) -> p c n", c=2)
            at += shape[0] * shape[1]
        xg, hh, hg, yy = parts["xg"], parts["hh"], parts["hg"], parts["yy"]
        xgT = parts["xgT"].rearrange("p c (k n) -> p c k n", k=KD)
        hgT = parts["hgT"].rearrange("p c (k n) -> p c k n", k=KI)
        bx_in, bt_ready, bT_done, bg_ready, bu_ready, bsilu, bh_done, bht_ready, bhT_done, by_ready, by_done, by_out = (
            [sem(f"bx_in{c}") for c in range(2)], sem("bt_ready"), sem("bT_done"), sem("bg_ready"), sem("bu_ready"),
            sem("bsilu"), sem("bh_done"), sem("bht_ready"), sem("bhT_done"), sem("by_ready"), sem("by_done"),
            [sem(f"by_out{c}") for c in range(2)])
        HB = NB // 2
        with nc.Block() as block:
            @block.sync
            def _(sp):
                def fetch(i, c):
                    wait(sp, bt_ready, 2 * i + c - 1)
                    sp.dma_start(xg[:, c, :], xg_dram[ds((2 * i + c) * P, P), :]).then_inc(bx_in[c], 16)

                def put(i, c):
                    wait(sp, by_done, 2 * i + c + 1)
                    sp.dma_start(yg_dram[ds((2 * i + c) * P, P), :], yy[:, c, :]).then_inc(by_out[c], 16)

                fetch(0, 0)
                fetch(0, 1)
                with sp.Fori(0, HB - 1) as i:
                    put(i, 0)
                    fetch(i + 1, 0)
                    put(i, 1)
                    fetch(i + 1, 1)
                put(HB - 1, 0)
                put(HB - 1, 1)
                for c in range(2):
                    sp.wait_ge(by_out[c], 16 * HB)

            @block.tensor
            def _(pe):
                pe.wait_ge(expert_in, 48)

                def transpose_x(i, c):
                    b = 2 * i + c
                    wait(pe, bx_in[c], 16 * i + 16)
                    wait(pe, bT_done, b)
                    for k in range(KD):
                        last = nc.tensor.transpose(psum[0][:, k * P:(k + 1) * P], xg[:, c, k * P:(k + 1) * P], mem["ident"][:, :])
                    last.then_inc(bt_ready, 1)

                def half(i, c, w, bank, done, taken, e):
                    b = 2 * i + c
                    wait(pe, bT_done, b + 1)
                    wait(pe, taken, b - 1)
                    for k in range(KD):
                        last = nc.tensor.matmul(psum[bank + c][:, 0:I], xgT[:, c, k, :], egu[:, k, ds(e * (2 * I) + w * I, I)],
                                                start=(k == 0), stop=(k == KD - 1))
                    last.then_inc(done, 1)

                def transpose_h(i, c):
                    b = 2 * i + c
                    wait(pe, bh_done, b + 1)
                    wait(pe, bhT_done, b)
                    for k in range(KI):
                        last = nc.tensor.transpose(psum[5][0:IR[k], k * P:(k + 1) * P], hh[:, c, k * P:k * P + IR[k]], mem["ident"][:, :])
                    last.then_inc(bht_ready, 1)

                def down(i, c, e):
                    b = 2 * i + c
                    wait(pe, bhT_done, b + 1)
                    wait(pe, by_done, b)
                    for k in range(KI):
                        last = nc.tensor.matmul(psum[6][:, 0:D], hgT[0:IR[k], c, k, :], edn[0:IR[k], k, ds(e * D, D)],
                                                start=(k == 0), stop=(k == KI - 1))
                    last.then_inc(by_ready, 1)

                def expert(i, c):
                    return pe.value_load(be[0:1, ds(2 * i + c, 1)], min_val=0, max_val=E - 1)

                def pair(i, last=False):
                    e0, e1 = expert(i, 0), expert(i, 1)
                    half(i, 0, 0, 1, bg_ready, bsilu, e0)
                    half(i, 0, 1, 3, bu_ready, bh_done, e0)
                    transpose_x(i, 1)
                    transpose_h(i, 0)
                    half(i, 1, 0, 1, bg_ready, bsilu, e1)
                    down(i, 0, e0)
                    half(i, 1, 1, 3, bu_ready, bh_done, e1)
                    if not last:
                        transpose_x(i + 1, 0)
                    transpose_h(i, 1)
                    down(i, 1, e1)

                transpose_x(0, 0)
                over_pairs(pe, HB - 1, pair)
                pair(HB - 1, True)

            @block.scalar
            def _(act):
                def copy_x(i, c):
                    b = 2 * i + c
                    wait(act, bt_ready, b + 1)
                    wait(act, bu_ready, b - 1)
                    nc.scalar.activation(xgT[:, c, :, :], psum[0][:, 0:D].rearrange("p (k n) -> p k n", k=KD), ACT.Copy).then_inc(bT_done, 1)

                def silu(i, c):
                    b = 2 * i + c
                    wait(act, bg_ready, b + 1)
                    wait(act, bh_done, b - 1)
                    nc.scalar.activation(hg[:, c, :], psum[1 + c][:, 0:I], ACT.Silu).then_inc(bsilu, 1)

                def copy_h(i, c):
                    b = 2 * i + c
                    wait(act, bht_ready, b + 1)
                    wait(act, by_ready, b - 1)
                    nc.scalar.activation(hgT[:, c, 0:2, :], psum[5][:, 0:2 * P].rearrange("p (k n) -> p k n", k=2), ACT.Copy)
                    nc.scalar.activation(hgT[0:IR[2], c, 2, :], psum[5][0:IR[2], 2 * P:3 * P], ACT.Copy).then_inc(bhT_done, 1)

                def pair(i, last):
                    silu(i, 0)
                    copy_x(i, 1)
                    copy_h(i, 0)
                    silu(i, 1)
                    if not last:
                        copy_x(i + 1, 0)
                    copy_h(i, 1)

                copy_x(0, 0)
                over_pairs(act, HB - 1, lambda i: pair(i, False))
                pair(HB - 1, True)

            @block.vector
            def _(dve):
                def hidden(i, c):
                    b = 2 * i + c
                    wait(dve, bsilu, b + 1)
                    wait(dve, bu_ready, b + 1)
                    wait(dve, bht_ready, b - 1)
                    nc.vector.tensor_tensor(hh[:, c, :], psum[3 + c][:, 0:I], hg[:, c, :], ALU.mult).then_inc(bh_done, 1)

                def take_y(i, c):
                    b = 2 * i + c
                    wait(dve, by_ready, b + 1)
                    if not isinstance(i, int) or i >= 1:
                        wait(dve, by_out[c], 16 * i)
                    nc.vector.tensor_copy(yy[:, c, :], psum[6][:, 0:D]).then_inc(by_done, 1)

                def pair(i):
                    for c in range(2):
                        hidden(i, c)
                        take_y(i, c)

                over_pairs(dve, HB, pair)

        kv_setup(nc, ctx, "kv1", mem, psum, wk, wv, attn1_in, 16 * 8, bcol[:, 1, :], bvrow, kb, vb)
        attention(nc, ctx, "attn1", mem, psum, x, wq[1], wo[1], kb, vb, bcol[:, 0, :], bo_all, attn1_in, 16 * 8,
                  combine={"w": wtop, "slot": slot, "y": yg_dram})

        fa = big[:, 0:KR * D].rearrange("p (k n) -> p k n", k=KR)
        fb = big[:, KR * D:2 * KR * D].rearrange("p (k n) -> p k n", k=KR)
        fbg = big[:, 2 * KR * D:(2 + B) * KR * D].rearrange("p (b k n) -> p b k n", b=B, k=KR)
        o0 = (2 + B) * KR * D
        wb = big[:, o0:o0 + B * KD * D].rearrange("p (b k n) -> p b k n", b=B, k=KD)
        o1 = o0 + B * KD * D
        xcol = big[:, o1:o1 + B * KD * P].rearrange("p (b k n) -> p b k n", b=B, k=KD)
        o2 = o1 + B * KD * P
        fo = big[:, o2:o2 + 2 * UT * D].rearrange("p (b t n) -> p b t n", b=2, t=UT)
        wr = sb("wr", [P, KD, E])
        gt = {n: sb("gt_" + n, [P, B, E]) for n in ("p", "key", "hot1", "rest", "hot2", "gate")}
        gc = {n: sb("gc_" + n, [P, B]) for n in ("top1", "top2", "kmax", "d", "e", "den", "inv")}
        gcol = sb("gcol", [P, B, KR])
        ln3 = LayerNorm(nc, ctx, "ln3", mem)
        f_xt, f_xT, f_col, f_lg, f_g, f_exp, f_gcol, f_scaled, f_w, f_wb, f_y, f_added, f_out, f_sum, f_dma = (
            sem(n) for n in ("f_xt", "f_xT", "f_col", "f_lg", "f_g", "f_exp", "f_gcol", "f_scaled", "f_w", "f_wb", "f_y",
                             "f_added", "f_out", "f_sum", "f_dma"))
        f_store = [sem(f"f_store{b}") for b in range(2)]
        out_t = out.rearrange("(t p) n -> p t n", p=P)
        with nc.Block() as block:
            @block.sync
            def _(sp):
                sp.dma_start(fa, a_in.rearrange("(k p) n -> p k n", p=P)).then_inc(ffn1_in, 16)
                sp.dma_start(fb, bw_in.rearrange("(k p) n -> p k n", p=P)).then_inc(ffn1_in, 16)
                sp.dma_start(wr[:, :, :], split(wr_in)).then_inc(ffn1_in, 16)
                with sp.Fori(0, NU // 2) as i:
                    for b in range(B):
                        wait(sp, f_out, 2 * i + b + 1)
                        sp.dma_start(out_t[:, ds(tile0(i, b), UT), :], fo[:, b, :, :]).then_inc(f_store[b], 16)
                for b in range(B):
                    sp.wait_ge(f_store[b], 16 * NU // 2)

            @block.gpsimd
            def _(pool):
                over_units(pool, lambda i, b, *_: ln3.rstd(pool, i, b))

            @block.tensor
            def _(pe):
                def front(i, b):
                    u = 2 * i + b
                    wait(pe, ln3.xn_ready, UT * u + UT)
                    wait(pe, f_xT, u - 1)
                    for t in range(UT):
                        for k in range(KD):
                            last = nc.tensor.transpose(psum[b][:, k * UN + t * P:k * UN + (t + 1) * P],
                                                       mem["xn"][:, b, t, k * P:(k + 1) * P], mem["ident"][:, :])
                    last.then_inc(f_xt, 1)

                def back(i, b):
                    u = 2 * i + b
                    wait(pe, f_xT, u + 1)
                    wait(pe, f_added, u - 1)
                    for t in range(UT):
                        for k in range(KD):
                            last = nc.tensor.matmul(psum[2 + b][:, t * D:(t + 1) * D], xTv[:, b, k, t * P:(t + 1) * P],
                                                    wb[:, b, k, :], start=(k == 0), stop=(k == KD - 1))
                    last.then_inc(f_y, 1)

                front(0, 0)
                front(0, 1)
                pe.wait_ge(ffn1_in, 48)
                pe.wait_ge(f_col, B * KD)
                for b in range(B):
                    for k in range(KD):
                        last = nc.tensor.matmul(psum[4][:, b * E:(b + 1) * E], xcol[:, b, k, :], wr[:, k, :],
                                                start=(k == 0), stop=(k == KD - 1))
                last.then_inc(f_lg, 1)
                pe.wait_ge(f_scaled, B * KR)
                for b in range(B):
                    for m in range(KD):
                        for k in range(KR):
                            last = nc.tensor.matmul(psum[6 + b][:, m * D:(m + 1) * D], fa[:, k, m * P:(m + 1) * P],
                                                    fbg[:, b, k, :], start=(k == 0), stop=(k == KR - 1))
                last.then_inc(f_w, 1)
                pe.wait_ge(f_wb, B)

                def pair(i):
                    for b in range(B):
                        back(i, b)
                        front(i + 1, b)

                over_pairs(pe, NU // 2 - 1, pair)
                for b in range(B):
                    back(NU // 2 - 1, b)

            @block.scalar
            def _(act):
                def copy(i, b):
                    u = 2 * i + b
                    wait(act, f_xt, u + 1)
                    wait(act, f_y, u - 1)
                    if isinstance(i, int) or True:
                        nc.scalar.activation(xTv[:, b, :, :], psum[b][:, :].rearrange("p (k n) -> p k n", k=KD),
                                             ACT.Copy).then_inc(f_xT, 1)
                copy(0, 0)
                copy(0, 1)
                act.wait_ge(f_g, 1)
                nc.scalar.activation(gc["e"][:, :], gc["d"][:, :], ACT.Exp).then_inc(f_exp, 1)
                act.wait_ge(f_w, 1)
                for b in range(B):
                    nc.scalar.activation(wb[:, b, :, :], psum[6 + b][:, :].rearrange("p (k n) -> p k n", k=KD),
                                         ACT.Copy).then_inc(f_wb, 1)
                with act.Fori(1, NU // 2) as i:
                    for b in range(B):
                        copy(i, b)

            @block.vector
            def _(dve):
                v = nc.vector

                def front(i, b):
                    ln3.stats(dve, x, i, b)
                    wait(dve, f_xt, 2 * i + b - 1)
                    wait(dve, f_added, 2 * i + b - 1)
                    ln3.normalise(dve, x, i, b)

                def back(i, b, later):
                    u = 2 * i + b
                    wait(dve, f_y, u + 1)
                    if later:
                        wait(dve, f_store[b], 16 * i)
                    v.tensor_tensor(fo[:, b, :, :], psum[2 + b][:, :].rearrange("p (t n) -> p t n", t=UT),
                                    mem["xn"][:, b, :, :], ALU.add).then_inc(f_added, 1)
                    wait(dve, f_added, u + 1)
                    v.tensor_tensor(fo[:, b, :, :], fo[:, b, :, :], x[:, ds(tile0(i, b), UT), :], ALU.add).then_inc(f_out, 1)

                front(0, 0)
                front(0, 1)
                dve.wait_ge(f_xT, 2)
                for b in range(B):
                    for k in range(KD):
                        v.tensor_copy(xcol[:, b, k, :], xTv[:, b, k, 0:1].to_broadcast([P, P])).then_inc(f_col, 1)
                dve.wait_ge(f_lg, 1)
                n = 0

                def link(ins):
                    nonlocal n
                    n += 1
                    ins.then_inc(f_sum, 1)
                    dve.wait_ge(f_sum, n)

                link(v.tensor_copy(gt["p"][:, :, :], psum[4][:, 0:B * E].rearrange("p (b e) -> p b e", b=B)))
                n = top_two(nc, dve, f_sum, n, gt["p"][:, :, :], rev[:, :].unsqueeze(1).to_broadcast([P, B, E]),
                            (gt["key"][:, :, :], gc["top1"][:, :], gt["hot1"][:, :, :], gt["rest"][:, :, :],
                             gc["top2"][:, :], gt["hot2"][:, :, :], gc["kmax"][:, :]), [P, B, E], -1e30)
                v.tensor_tensor(gc["d"][:, :], gc["top2"][:, :], gc["top1"][:, :], ALU.subtract).then_inc(f_g, 1)
                dve.wait_ge(f_exp, 1)
                link(v.tensor_scalar(gc["den"][:, :], gc["e"][:, :], 1.0, None, ALU.add))
                link(v.reciprocal(gc["inv"][:, :], gc["den"][:, :]))
                wide = lambda a: a.unsqueeze(2).to_broadcast([P, B, E])
                link(v.tensor_tensor(gt["gate"][:, :, :], gt["hot2"][:, :, :], wide(gc["e"][:, :]), ALU.mult))
                link(v.tensor_tensor(gt["gate"][:, :, :], gt["gate"][:, :, :], gt["hot1"][:, :, :], ALU.add))
                link(v.tensor_tensor(gt["gate"][:, :, :], gt["gate"][:, :, :], wide(gc["inv"][:, :]), ALU.mult))
                for b in range(B):
                    pairs = gt["gate"][:, b, :].rearrange("p (k q) -> p k q", q=2)
                    for q in range(2):
                        v.tensor_copy(gcol[q * R:(q + 1) * R, b, :], pairs[q * R:(q + 1) * R, :, q]).then_inc(f_gcol, 1)
                dve.wait_ge(f_gcol, 2 * B)
                dve.wait_ge(ffn1_in, 48)
                for b in range(B):
                    for k in range(KR):
                        v.tensor_scalar(fbg[:, b, k, :], fb[:, k, :], gcol[:, b, k:k + 1], None, ALU.mult).then_inc(f_scaled, 1)
                back(0, 0, False)
                front(1, 0)
                back(0, 1, False)
                front(1, 1)
                with dve.Fori(1, NU // 2 - 1) as i:
                    for b in range(B):
                        back(i, b, True)
                        front(i + 1, b)
                for b in range(B):
                    back(NU // 2 - 1, b, True)
                dve.wait_ge(f_out, NU)


def kernel(**inputs):
    import numpy as np
    import concourse.bacc as bacc
    from concourse import mybir as mb
    from concourse.bass_utils import run_bass_kernel_spmd as run

    g = {k: np.asarray(v) for k, v in inputs.items()}
    nb, ns, nd = g["x"].shape
    ne, ni2 = g["L0_ffn_experts_gate_up"].shape[:2]
    ni = g["L0_ffn_experts_down"].shape[2]
    nr = g["L1_ffn_A"].shape[1]
    laid = [
        ("x", g["x"].reshape(nb * ns, nd)),
        ("ctxT", g["ctx_1024"].reshape(-1, nd).T),
        ("wq0", g["L0_xattn_W_q"].T), ("wk0", g["L0_xattn_W_k"].T), ("wv0", g["L0_xattn_W_v"].T), ("wo0", g["L0_xattn_W_fc"].T),
        ("gate", np.concatenate([g["L0_ffn_gate_w"], g["L0_ffn_shared_expert_gate_w"]], axis=0).T),
        ("egu", g["L0_ffn_experts_gate_up"].transpose(2, 0, 1).reshape(nd, ne * ni2)),
        ("edown", g["L0_ffn_experts_down"].transpose(2, 0, 1).reshape(ni, ne * nd)),
        ("sgate", g["L0_ffn_shared_gate_w"].T), ("sup", g["L0_ffn_shared_up_w"].T), ("sdown", g["L0_ffn_shared_down_w"].T),
        ("wq1", g["L1_xattn_Wq"]), ("bq1", g["L1_xattn_bq"]), ("wk1", g["L1_xattn_Wk"]), ("bk1", g["L1_xattn_bk"]),
        ("wv1", g["L1_xattn_Wv"]), ("bv1", g["L1_xattn_bv"]), ("wo1", g["L1_xattn_Wo"]), ("bo1", g["L1_xattn_bo"]),
        ("wr", g["L1_ffn_Wr"].T), ("a", g["L1_ffn_A"].reshape(ne * nr, nd)),
        ("bw", g["L1_ffn_Bw"].transpose(0, 2, 1).reshape(ne * nr, nd)),
    ]
    nc = bacc.Bacc("TRN2", target_bir_lowering=False, num_devices=1)
    arrays, args = {}, []
    for name, a in laid:
        a = np.ascontiguousarray(a)
        arrays[f"in_{name}"] = a
        args.append(nc.dram_tensor(f"in_{name}", a.shape, mb.dt.from_np(a.dtype), kind="ExternalInput").ap())
    out = nc.dram_tensor("out_x", (nb * ns, nd), mb.dt.float32, kind="ExternalOutput").ap()
    xattn_ffn_kernel(nc, *args, out)
    r = run(nc, [arrays], core_ids=[0])
    return r.results[0]["out_x"].reshape(nb, ns, nd)
```

```python
import concourse.bass as bass
from concourse import mybir
from contextlib import ExitStack

F32 = mybir.dt.float32
I32 = mybir.dt.int32
ALU = mybir.AluOpType
ACT = mybir.ActivationFunctionType
AX = mybir.AxisListType
ds = bass.ds

P = 128
B, S, D = 2, 1024, 256
NT = B * S // P
TB = NT // B
KD = D // P
UT = 2
UN = UT * P
NU = NT // UT
H, DH, SK = 16, 16, 64
HH = H // 2
E, I = 8, 352
KI = 3
IR = [P, P, I - 2 * P]
SI = 704
KS = 6
SR = [P] * 5 + [SI - 5 * P]
SG = 512
NP = H // 2
NB = 40
SLOTS = NB * P
R = 64
KR = E * R // P
EPS = 1e-5
SCALE = DH ** -0.5


def wait(engine, sem, value):
    if isinstance(value, int) and value <= 0:
        return
    engine.wait_ge(sem, value)


def tile0(i, b):
    return 2 * i + TB * b


def over_units(engine, unit):
    for b in range(B):
        unit(0, b, True, False)
    with engine.Fori(1, NU // 2 - 1) as i:
        for b in range(B):
            unit(i, b, False, False)
    for b in range(B):
        unit(NU // 2 - 1, b, False, True)


def over_pairs(engine, n, pair):
    pair(0)
    with engine.Fori(1, n) as i:
        pair(i)


class LayerNorm:

    def __init__(self, nc, ctx, name, mem):
        self.nc, self.mem = nc, mem
        self.stats_done = ctx.enter_context(nc.semaphore(name + "_stats_done"))
        self.mean_done = ctx.enter_context(nc.semaphore(name + "_mean_done"))
        self.var_ready = ctx.enter_context(nc.semaphore(name + "_var_ready"))
        self.rstd_ready = ctx.enter_context(nc.semaphore(name + "_rstd_ready"))
        self.xn_ready = ctx.enter_context(nc.semaphore(name + "_xn_ready"))

    def carry_wait(self, n):
        self.nc.vector.memset(self.mem["carry"][:, n:n + 1], 0.0)

    def stats(self, dve, x, i, b):
        u, m, nc = 2 * i + b, self.mem, self.nc
        for t in range(UT):
            nc.vector.bn_stats(m["stats"][:, b, t, :], x[:, ds(tile0(i, b) + t, 1), :]).then_inc(self.stats_done, 1)
        wait(dve, self.stats_done, UT * u + UT)
        self.carry_wait(0)
        for t in range(UT):
            nc.vector.bn_aggr(m["mv"][:, b, t, :], m["stats"][:, b, t, :]).then_inc(self.mean_done, 1)
        wait(dve, self.mean_done, UT * u + UT)
        wait(dve, self.rstd_ready, 2 * u - 2)
        nc.vector.tensor_scalar(m["nmean"][:, b, :], m["mv"][:, b, :, 0], -1.0, None, ALU.mult).then_inc(self.var_ready, 1)
        nc.vector.tensor_scalar(m["var"][:, b, :], m["mv"][:, b, :, 1], EPS, None, ALU.add).then_inc(self.var_ready, 1)

    def rstd(self, pool, i, b):
        u, m, nc = 2 * i + b, self.mem, self.nc
        wait(pool, self.var_ready, UT * u + UT)
        nc.gpsimd.tensor_tensor(m["rstd"][:, b, :], m["var"][:, b, :], m["mhalf"][:, :], ALU.pow).then_inc(self.rstd_ready, 1)
        wait(pool, self.rstd_ready, 2 * u + 1)
        nc.gpsimd.tensor_tensor(m["shift"][:, b, :], m["nmean"][:, b, :], m["rstd"][:, b, :], ALU.mult).then_inc(self.rstd_ready, 1)

    def normalise(self, act, x, i, b):
        u, m, nc = 2 * i + b, self.mem, self.nc
        wait(act, self.rstd_ready, 2 * u + 2)
        for t in range(UT):
            nc.scalar.activation(m["xn"][:, b, t, :], x[:, ds(tile0(i, b) + t, 1), :].squeeze(1), ACT.Identity,
                                 bias=m["shift"][:, b, t:t + 1], scale=m["rstd"][:, b, t:t + 1]).then_inc(self.xn_ready, 1)


def kv_setup(nc, ctx, name, mem, psum, wk, wv, wsem, wcount, bk, bv, kb, vb):
    kT_ready = ctx.enter_context(nc.semaphore(name + "_kT_ready"))
    kT_sb = ctx.enter_context(nc.semaphore(name + "_kT_sb"))
    v_ready = ctx.enter_context(nc.semaphore(name + "_v_ready"))
    vb_zero = ctx.enter_context(nc.semaphore(name + "_vb_zero"))
    kv_done = ctx.enter_context(nc.semaphore(name + "_kv_done"))
    psK = psum[0][:, :].rearrange("p (h n) -> p h n", h=KD)[:, :, 0:B * SK]
    psV = psum[1][:, :].rearrange("p (b n) -> p b n", b=B)

    with nc.Block() as block:
        @block.tensor
        def _(pe):
            pe.wait_ge(wsem, wcount)
            for hf in range(KD):
                for k in range(KD):
                    last = nc.tensor.matmul(psK[:, hf, :], wk[:, k, hf * P:(hf + 1) * P], mem["ctxT"][:, k, 0, :],
                                            start=(k == 0), stop=(k == KD - 1))
            last.then_inc(kT_ready, 1)
            for b in range(B):
                for k in range(KD):
                    last = nc.tensor.matmul(psV[:, b, :], mem["ctxT"][:, k, 1 + b, :], wv[:, k, :],
                                            start=(k == 0), stop=(k == KD - 1 and bv is None))
                if bv is not None:
                    last = nc.tensor.matmul(psV[:, b, :], mem["ones_row"][0:1, :], bv[0:1, :], start=False, stop=True)
            last.then_inc(v_ready, 1)

        @block.scalar
        def _(act):
            act.wait_ge(kT_ready, 1)
            for hf in range(KD):
                if bk is None:
                    nc.scalar.activation(mem["kT"][:, hf, :], psK[:, hf, :], ACT.Copy).then_inc(kT_sb, 1)
                else:
                    nc.scalar.activation(mem["kT"][:, hf, :], psK[:, hf, :], ACT.Identity,
                                         bias=bk[:, hf:hf + 1]).then_inc(kT_sb, 1)

        @block.vector
        def _(dve):
            for b in range(B):
                nc.vector.memset(vb[b][:, :, :], 0.0).then_inc(vb_zero, 1)
            dve.wait_ge(vb_zero, B)
            dve.wait_ge(v_ready, 1)
            n = 0
            for b in range(B):
                for h2 in range(2):
                    rows = slice(h2 * SK, (h2 + 1) * SK)
                    at = slice(h2 * DH, (h2 + 1) * DH)
                    src = psV[rows, b, :].rearrange("p (j c) -> p j c", j=NP)
                    nc.vector.tensor_copy(vb[b][rows, :, at], src[:, :, at]).then_inc(kv_done, 1)
                    n += 1
            dve.wait_ge(kT_sb, KD)
            for b in range(B):
                for hf in range(KD):
                    nc.vector.tensor_tensor(
                        kb[b][:, hf, :].rearrange("p (h k) -> p h k", h=HH),
                        mem["kT"][:, hf, b * SK:(b + 1) * SK].unsqueeze(1).to_broadcast([P, HH, SK]),
                        mem["head_of_row"][:, :].unsqueeze(2).to_broadcast([P, HH, SK]), ALU.mult).then_inc(kv_done, 1)
                    n += 1
            dve.wait_ge(kv_done, n)


def attention(nc, ctx, name, mem, psum, x, wq, wo, kb, vb, bq, bo, x_ready, x_count, combine=None):
    sem = lambda n: ctx.enter_context(nc.semaphore(f"{name}_{n}"))
    ln = LayerNorm(nc, ctx, name, mem)
    xt_ready, xT_ready, q_ready, qT_ready = sem("xt_ready"), sem("xT_ready"), sem("q_ready"), sem("qT_ready")
    s_ready, max_done, sub_done, exp_done = sem("s_ready"), sem("max_done"), sem("sub_done"), sem("exp_done")
    sum_done, inv_ready, pn_ready = sem("sum_done"), sem("inv_ready"), sem("pn_ready")
    t_ready, pT_ready, av_ready, oT_ready = sem("t_ready"), sem("pT_ready"), sem("av_ready"), sem("oT_ready")
    wo_ready, resid_done, bias_done = sem("wo_ready"), sem("resid_done"), sem("bias_done")
    y1_added, y2_added, y_here = sem("y1_added"), sem("y2_added"), [sem(f"y_here{b}") for b in range(2)]
    psXT = psum[0][:, :].rearrange("p (k n) -> p k n", k=KD)
    psQ = psum[1][:, :].rearrange("p (k n) -> p k n", k=KD)
    psS = [psum[2], psum[3]]
    psT = [psum[4], psum[5]]
    psO = psum[6][:, :].rearrange("p (k n) -> p k n", k=KD)
    psW = psum[7][:, :].rearrange("p (t n) -> p t n", t=UT)
    xn, xT, qT, pw, pT, oT = mem["xn"], mem["xT"], mem["qT"], mem["pw"], mem["pT"], mem["oT"]
    pairs = NU // 2

    def program(engine, steps, before, after):
        def unit(i, b, first, last):
            prev = None if first and b == 0 else ((i, 0) if b else (i - 1, 1))
            prev2 = None if first else (i - 1, b)
            nxt = None if last and b == 1 else ((i, 1) if b == 0 else (i + 1, 0))
            for s in range(4):
                steps(i, b, s, prev, prev2, nxt)
        before()
        over_units(engine, unit)
        after()

    with nc.Block() as block:
        @block.tensor
        def _(pe):
            def transpose_x(i, b):
                u = 2 * i + b
                wait(pe, ln.xn_ready, UT * u + UT)
                wait(pe, xT_ready, u)
                for t in range(UT):
                    for k in range(KD):
                        last = nc.tensor.transpose(psXT[:, k, t * P:(t + 1) * P], xn[:, b, t, k * P:(k + 1) * P],
                                                   mem["ident"][:, :])
                last.then_inc(xt_ready, 1)

            def project_q(i, b):
                u = 2 * i + b
                wait(pe, xT_ready, u + 1)
                wait(pe, qT_ready, KD * u)
                for hf in range(KD):
                    for k in range(KD):
                        last = nc.tensor.matmul(psQ[:, hf, :], wq[:, k, hf * P:(hf + 1) * P], xT[:, b, k, :],
                                                start=(k == 0), stop=(k == KD - 1))
                last.then_inc(q_ready, 1)

            def scores(i, b, s):
                u = 2 * i + b
                t, hf = s // 2, s % 2
                wait(pe, qT_ready, KD * u + KD)
                wait(pe, sub_done, 4 * u + s - 1)
                nc.tensor.matmul(psS[s % 2][:, :], qT[:, b, hf, t * P:(t + 1) * P], kb[b][:, hf, :],
                                 start=True, stop=True).then_inc(s_ready, 1)

            def transpose_p(i, b, s):
                u = 2 * i + b
                wait(pe, pn_ready, 4 * u + s + 1)
                wait(pe, pT_ready, 4 * u + s - 1)
                for j in range(4):
                    last = nc.tensor.transpose(psT[s % 2][:, j * P:(j + 1) * P], pw[:, s, j * P:(j + 1) * P],
                                               mem["ident"][:, :])
                last.then_inc(t_ready, 1)

            def values(i, b):
                u = 2 * i + b
                wait(pe, pT_ready, 4 * u + 4)
                wait(pe, oT_ready, u)
                for k in range(KD):
                    for j in range(4):
                        last = nc.tensor.matmul(psO[32 * j:32 * j + 32, k, :], vb[b][:, 4 * k + j, :],
                                                pT[:, b, 4 * k + j, :], start=True, stop=True,
                                                tile_position=(0, 32 * j))
                last.then_inc(av_ready, 1)

            def project_o(i, b):
                u = 2 * i + b
                wait(pe, oT_ready, u + 1)
                wait(pe, resid_done, u)
                for t in range(UT):
                    for k in range(KD):
                        last = nc.tensor.matmul(psW[:, t, :], oT[:, b, k, t * P:(t + 1) * P], wo[:, k, :],
                                                start=(k == 0), stop=(k == KD - 1))
                last.then_inc(wo_ready, 1)

            def steps(i, b, s, prev, prev2, nxt):
                scores(i, b, s)
                if s == 3 and nxt:
                    project_q(*nxt)
                if s == 3:
                    transpose_p(i, b, 0)
                elif prev:
                    transpose_p(*prev, s + 1)
                if s == 1 and prev2:
                    project_o(*prev2)
                if s == 2 and nxt:
                    transpose_x(*nxt)
                if s == 3 and prev:
                    values(*prev)

            def before():
                transpose_x(0, 0)
                project_q(0, 0)

            def after():
                transpose_p(pairs - 1, 1, 1)
                project_o(pairs - 1, 0)
                transpose_p(pairs - 1, 1, 2)
                transpose_p(pairs - 1, 1, 3)
                values(pairs - 1, 1)
                project_o(pairs - 1, 1)

            program(pe, steps, before, after)

        @block.scalar
        def _(act):
            def normalise(i, b):
                wait(act, xt_ready, 2 * i + b - 1)
                ln.normalise(act, x, i, b)

            def copy_xT(i, b):
                u = 2 * i + b
                wait(act, xt_ready, u + 1)
                wait(act, q_ready, u - 1)
                nc.scalar.activation(xT[:, b, :, :], psXT[:, :, :], ACT.Copy).then_inc(xT_ready, 1)

            def copy_q(i, b):
                u = 2 * i + b
                wait(act, q_ready, u + 1)
                wait(act, s_ready, 4 * u - 4)
                for hf in range(KD):
                    if bq is None:
                        nc.scalar.activation(qT[:, b, hf, :], psQ[:, hf, :], ACT.Copy).then_inc(qT_ready, 1)
                    else:
                        nc.scalar.activation(qT[:, b, hf, :], psQ[:, hf, :], ACT.Identity,
                                             bias=bq[:, hf:hf + 1]).then_inc(qT_ready, 1)

            def exps(i, b, s):
                wait(act, sub_done, 4 * (2 * i + b) + s + 1)
                nc.scalar.activation(pw[:, s, :], pw[:, s, :], ACT.Exp, scale=SCALE).then_inc(exp_done, 1)

            def copy_pT(i, b, s):
                u = 2 * i + b
                t, hf = s // 2, s % 2
                wait(act, t_ready, 4 * u + s + 1)
                wait(act, av_ready, u - 1)
                nc.scalar.activation(pT[:, b, hf * 4:(hf + 1) * 4, t * P:(t + 1) * P],
                                     psT[s % 2][:, :].rearrange("p (j n) -> p j n", j=4), ACT.Copy).then_inc(pT_ready, 1)

            def copy_o(i, b):
                u = 2 * i + b
                wait(act, av_ready, u + 1)
                wait(act, wo_ready, u - 1)
                nc.scalar.activation(oT[:, b, :, :], psO[:, :, :], ACT.Copy).then_inc(oT_ready, 1)

            def steps(i, b, s, prev, prev2, nxt):
                if s == 3:
                    exps(i, b, s)
                    if nxt:
                        copy_q(*nxt)
                    copy_pT(i, b, 0)
                    if prev:
                        copy_o(*prev)
                else:
                    if prev:
                        copy_pT(*prev, s + 1)
                    exps(i, b, s)
                if s == 1 and nxt:
                    normalise(*nxt)
                if s == 2 and nxt:
                    copy_xT(*nxt)

            def before():
                normalise(0, 0)
                copy_xT(0, 0)
                copy_q(0, 0)

            def after():
                for s in (1, 2, 3):
                    copy_pT(pairs - 1, 1, s)
                copy_o(pairs - 1, 1)

            program(act, steps, before, after)

        @block.vector
        def _(dve):
            heads = lambda a: a.rearrange("p (h k) -> p h k", h=HH)

            def shift(i, b, s):
                u = 2 * i + b
                mx = mem["mx"][:, s % 2, :]
                wait(dve, s_ready, 4 * u + s + 1)
                nc.vector.tensor_reduce(mx, heads(psS[s % 2][:, :]), AX.X, ALU.max).then_inc(max_done, 1)
                wait(dve, max_done, 4 * u + s + 1)
                wait(dve, t_ready, 4 * u + s - 3)
                nc.vector.tensor_tensor(heads(pw[:, s, :]), heads(psS[s % 2][:, :]),
                                        mx.unsqueeze(2).to_broadcast([P, HH, SK]), ALU.subtract).then_inc(sub_done, 1)

            def weight_sums(i, b, s):
                n = 4 * (2 * i + b) + s
                wait(dve, exp_done, n + 1)
                nc.vector.tensor_reduce(mem["wsum"][:, s, :], heads(pw[:, s, :]), AX.X, ALU.add).then_inc(sum_done, 1)
                wait(dve, sum_done, n + 1)
                nc.vector.reciprocal(mem["winv"][:, s, :], mem["wsum"][:, s, :]).then_inc(inv_ready, 1)

            def residual(i, b):
                u = 2 * i + b
                wait(dve, wo_ready, u + 1)
                if bo is not None:
                    wait(dve, bias_done, UT * u + UT)
                rows = x[:, ds(tile0(i, b), UT), :]
                nc.vector.tensor_tensor(rows, psW[:, :, :], rows, ALU.add).then_inc(resid_done, 1)

            def norm_first(i, b):
                u = 2 * i + b
                if combine is not None:
                    wait(dve, y_here[b], 64 * i + 64)
                    for j in range(2):
                        for t in range(UT):
                            rows = x[:, ds(tile0(i, b) + t, 1), :].squeeze(1)
                            nc.vector.scalar_tensor_tensor(rows, mem["yg"][:, b, t, j, :],
                                                           combine["w"][:, j, ds(tile0(i, b) + t, 1)], rows,
                                                           ALU.mult, ALU.add).then_inc((y1_added, y2_added)[j], 1)
                        wait(dve, (y1_added, y2_added)[j], UT * u + UT)
                    ln.carry_wait(1)
                ln.stats(dve, x, i, b)

            def steps(i, b, s, prev, prev2, nxt):
                shift(i, b, s)
                if s >= 1:
                    weight_sums(i, b, s - 1)
                elif prev:
                    weight_sums(*prev, 3)
                if s == 0 and nxt:
                    norm_first(*nxt)
                if s == 2 and prev2:
                    residual(*prev2)

            def before():
                wait(dve, x_ready, x_count)
                norm_first(0, 0)

            def after():
                weight_sums(pairs - 1, 1, 3)
                residual(pairs - 1, 0)
                residual(pairs - 1, 1)
                dve.wait_ge(resid_done, NU)

            program(dve, steps, before, after)

        @block.gpsimd
        def _(pool):
            def gather(i, b):
                wait(pool, y2_added, UT * (2 * i + b - 1))
                for t in range(UT):
                    for j in range(2):
                        tl = tile0(i, b) + t
                        pool.indirect_dma_start(mem["yg"][:, b, t, j, :], None, combine["y"][:, :],
                                                bass.IndirectOffsetOnAxis(ap=combine["slot"][:, j, tl:tl + 1], axis=0),
                                                bounds_check=SLOTS - 1).then_inc(y_here[b], 16)

            def normalise_weights(i, b, s):
                wait(pool, inv_ready, 4 * (2 * i + b) + s + 1)
                view = pw[:, s, :].rearrange("p (h k) -> p h k", h=HH)
                nc.gpsimd.tensor_tensor(view, view, mem["winv"][:, s, :].unsqueeze(2).to_broadcast([P, HH, SK]),
                                        ALU.mult).then_inc(pn_ready, 1)

            def add_bias(i, b):
                wait(pool, ln.xn_ready, UT * (2 * i + b) + UT)
                for t in range(UT):
                    rows = x[:, ds(tile0(i, b) + t, 1), :].squeeze(1)
                    nc.gpsimd.tensor_tensor(rows, rows, bo[:, :], ALU.add).then_inc(bias_done, 1)

            def steps(i, b, s, prev, prev2, nxt):
                if s >= 1:
                    normalise_weights(i, b, s - 1)
                elif prev:
                    normalise_weights(*prev, 3)
                if s == 0 and nxt:
                    ln.rstd(pool, *nxt)
                if s == 2 and nxt and bo is not None:
                    add_bias(*nxt)

            def before():
                if combine is not None:
                    gather(0, 0)
                ln.rstd(pool, 0, 0)
                if bo is not None:
                    add_bias(0, 0)
                if combine is not None:
                    gather(0, 1)

            def after():
                normalise_weights(pairs - 1, 1, 3)

            if combine is None:
                program(pool, steps, before, after)
            else:
                before()
                for i in range(pairs):
                    for b in range(B):
                        prev = None if i + b == 0 else ((i, 0) if b else (i - 1, 1))
                        nxt = None if (i, b) == (pairs - 1, 1) else ((i, 1) if b == 0 else (i + 1, 0))
                        for s in range(4):
                            steps(i, b, s, prev, None, nxt)
                            if s == 3 and i + 1 < pairs:
                                gather(i + 1, b)
                after()


def top_two(nc, dve, sem, base, p, rev, work, shape, low):
    key, top1, hot1, rest, top2, hot2, kmax = work
    n = base

    def link(ins):
        nonlocal n
        n += 1
        ins.then_inc(sem, 1)
        dve.wait_ge(sem, n)

    wide = lambda a: a.unsqueeze(len(shape) - 1).to_broadcast(shape)
    v = nc.vector
    for src, top, hot in ((p, top1, hot1), (rest, top2, hot2)):
        link(v.tensor_reduce(top, src, AX.X, ALU.max))
        link(v.tensor_tensor(key, src, wide(top), ALU.is_equal))
        link(v.tensor_tensor(key, key, rev, ALU.mult))
        link(v.tensor_reduce(kmax, key, AX.X, ALU.max))
        link(v.tensor_tensor(hot, key, wide(kmax), ALU.is_equal))
        if src is p:
            link(v.scalar_tensor_tensor(rest, hot, low, p, ALU.mult, ALU.add))
    return n


def xattn_ffn_kernel(nc, x_in, ctxT_in, wq0, wk0, wv0, wo0, gate_in, egu_in, edown_in, sgate_in, sup_in, sdown_in,
                     wq1, bq1, wk1, bk1, wv1, bv1, wo1, bo1, wr_in, a_in, bw_in, out):
    ctx = ExitStack()
    with ctx:
        def sb(name, shape, dt=F32):
            return ctx.enter_context(nc.sbuf_tensor(name, shape, dt))

        def sem(name):
            return ctx.enter_context(nc.semaphore(name))

        psum = [ctx.enter_context(nc.psum_tensor(f"bank{n}", [P, 512], F32)) for n in range(8)]
        xg_dram = nc.dram_tensor("expert_rows_in", [SLOTS, D], F32, kind="Internal").ap()
        yg_dram = nc.dram_tensor("expert_rows_out", [SLOTS, D], F32, kind="Internal").ap()

        x = sb("x", [P, NT, D])
        xn2 = sb("xn2", [P, NT, D])
        mem = {
            "ident": sb("ident", [P, P]), "ones_row": sb("ones_row", [1, P]),
            "head_of_row": sb("head_of_row", [P, HH]), "ctxT": sb("ctxT", [P, KD, 1 + B, P]),
            "kT": sb("kT", [P, KD, B * SK]),
            "stats": sb("stats", [P, 2, UT, 6]), "mv": sb("mv", [P, 2, UT, 2]), "var": sb("var", [P, 2, UT]),
            "rstd": sb("rstd", [P, 2, UT]), "nmean": sb("nmean", [P, 2, UT]), "shift": sb("shift", [P, 2, UT]), "carry": sb("carry", [P, 2]), "mhalf": sb("mhalf", [P, UT]),
            "xn": sb("xn", [P, 2, UT, D]), "xT": sb("xT", [P, 2, KD, UN]), "qT": sb("qT", [P, 2, KD, UN]),
            "mx": sb("mx", [P, 2, HH]), "pw": sb("pw", [P, 4, 512]), "wsum": sb("wsum", [P, 4, HH]),
            "winv": sb("winv", [P, 4, HH]),
        }
        big = sb("big", [P, 13 * 512])
        mem["pT"] = xn2[:, :, :].rearrange("p (b j) n -> p b j n", b=2)
        mem["oT"] = big[:, 0:1024].rearrange("p (b k n) -> p b k n", b=2, k=KD)
        mem["yg"] = big[:, 1024:3072].rearrange("p (b t j n) -> p b t j n", b=2, t=UT, j=2)
        wq = [sb("wq", [P, KD, D])] * 2
        wo = [sb("wo", [P, KD, D])] * 2
        wk = sb("wk", [P, KD, D])
        wv = sb("wv", [P, KD, D])
        kvb = sb("kvb", [P, 8 * 512])
        kb = [kvb[:, b * 1024:(b + 1) * 1024].rearrange("p (h n) -> p h n", h=KD) for b in range(B)]
        vb = [kvb[:, 2048 + b * 256:2048 + (b + 1) * 256].rearrange("p (j n) -> p j n", j=NP) for b in range(B)]
        bcol = sb("bcol", [P, 2, KD])
        bvrow = sb("bvrow", [1, D])
        zeros = sb("zeros", [P, D])
        bo_all = sb("bo_all", [P, D])
        gw = sb("gw", [P, KD, E + 1])
        egu = sb("egu", [P, KD, E * 2 * I])
        edn = sb("edn", [P, KI, E * D])
        sgu = sb("sgu", [P, 2, KD, SI])
        sdn = sb("sdn", [P, KS, D])

        x_in_done, attn0_in, attn1_in, router_in, shared_in, expert_in, ffn1_in = (
            sem("x_in_done"), sem("attn0_in"), sem("attn1_in"), sem("router_in"), sem("shared_in"), sem("expert_in"), sem("ffn1_in"))
        made, zero_made, rows_zeroed = sem("made"), sem("zero_made"), sem("rows_zeroed")
        split = lambda a: a.rearrange("(k p) n -> p k n", p=P)
        with nc.Block() as block:
            @block.sync
            def _(sp):
                sp.dma_start(mem["ctxT"][:, :, 0, :], split(ctxT_in)).then_inc(attn0_in, 16)
                for b in range(B):
                    for c in range(2):
                        sp.dma_start(mem["ctxT"][:, :, 1 + b, c * SK:(c + 1) * SK],
                                     split(ctxT_in)[:, :, b * SK:(b + 1) * SK]).then_inc(attn0_in, 16)
                sp.dma_start(wk[:, :, :], split(wk0)).then_inc(attn0_in, 16)
                sp.dma_start(wv[:, :, :], split(wv0)).then_inc(attn0_in, 16)
                sp.dma_start(wq[0][:, :, :], split(wq0)).then_inc(attn0_in, 16)
                sp.dma_start(wo[0][:, :, :], split(wo0)).then_inc(attn0_in, 16)
                sp.dma_start(gw[:, :, :], split(gate_in)).then_inc(router_in, 16)
                sp.dma_start(sgu[:, 0, :, :], split(sgate_in)).then_inc(shared_in, 16)
                sp.dma_start(sgu[:, 1, :, :], split(sup_in)).then_inc(shared_in, 16)
                sp.dma_start(sdn[:, 0:5, :], split(sdown_in[0:5 * P, :])).then_inc(shared_in, 16)
                sp.dma_start(sdn[0:SR[5], 5, :], sdown_in[5 * P:SI, :]).then_inc(shared_in, 16)
                sp.wait_ge(zero_made, 1)
                sp.dma_start(xg_dram.rearrange("(c p) d -> p c d", p=P), 
                             zeros[:, :].unsqueeze(1).to_broadcast([P, NB, D])).then_inc(rows_zeroed, 16)

            @block.scalar
            def _(act):
                for c in range(4):
                    act.dma_start(x[:, 4 * c:4 * c + 4, :],
                                  x_in[4 * c * P:(4 * c + 4) * P, :].rearrange("(t p) n -> p t n", p=P)).then_inc(x_in_done, 16)
                act.dma_start(egu[:, :, :], split(egu_in)).then_inc(expert_in, 16)
                act.dma_start(edn[:, 0:2, :], split(edown_in[0:2 * P, :])).then_inc(expert_in, 16)
                act.dma_start(edn[0:IR[2], 2, :], edown_in[2 * P:I, :]).then_inc(expert_in, 16)

            @block.vector
            def _(dve):
                nc.vector.memset(zeros[:, :], 0.0).then_inc(zero_made, 1)
                nc.vector.memset(mem["ones_row"][:, :], 1.0).then_inc(made, 1)
                nc.vector.memset(mem["mhalf"][:, :], -0.5).then_inc(made, 1)

            @block.gpsimd
            def _(pool):
                nc.gpsimd.memset(mem["ident"][:, :], 0.0).then_inc(made, 1)
                nc.gpsimd.memset(mem["head_of_row"][:, :], 1.0).then_inc(made, 1)
                pool.wait_ge(made, 4)
                nc.gpsimd.affine_select(out=mem["ident"][:, :], in_=mem["ident"][:, :], compare_op=ALU.not_equal, fill=1.0,
                                        base=0, pattern=[[-1, P]], channel_multiplier=1).then_inc(made, 1)
                nc.gpsimd.affine_select(out=mem["head_of_row"][:, :], in_=mem["head_of_row"][:, :], compare_op=ALU.is_ge,
                                        fill=0.0, base=0, pattern=[[-DH, HH]], channel_multiplier=1).then_inc(made, 1)
                pool.wait_ge(made, 6)
                nc.gpsimd.affine_select(out=mem["head_of_row"][:, :], in_=mem["head_of_row"][:, :], compare_op=ALU.is_ge,
                                        fill=0.0, base=DH - 1, pattern=[[DH, HH]], channel_multiplier=-1).then_inc(made, 1)
                pool.wait_ge(made, 7)

        kv_setup(nc, ctx, "kv0", mem, psum, wk, wv, attn0_in, 16 * 9, None, None, kb, vb)
        attention(nc, ctx, "attn0", mem, psum, x, wq[0], wo[0], kb, vb, None, None, x_in_done, 64)

        xn2T = kvb[:, :].rearrange("p (k n) -> p k n", k=KD)
        lg = sb("lg", [P, NT, E + 1])
        ln = LayerNorm(nc, ctx, "ln2", mem)
        xt_ready, xT_ready, xT2_ready, kept, lg_ready, lg_taken = (
            sem("r_xt_ready"), sem("r_xT_ready"), sem("r_xT2_ready"), sem("r_kept"), sem("r_lg_ready"), sem("r_lg_taken"))
        xTv = mem["xT"]
        with nc.Block() as block:
            @block.sync
            def _(sp):
                for dst, src in ((wk, wk1), (wv, wv1), (wq[1], wq1), (wo[1], wo1)):
                    sp.dma_start(dst[:, :, :], split(src)).then_inc(attn1_in, 16)
                for n, src in enumerate((bq1, bk1)):
                    sp.dma_start(bcol[:, n, :], src.rearrange("(k p) -> p k", p=P),
                                 allow_slow_non_contiguous=True).then_inc(attn1_in, 16)
                sp.dma_start(bvrow[:, :], bv1.rearrange("(a n) -> a n", a=1)).then_inc(attn1_in, 16)
                sp.dma_start(bo_all[:, :], bo1.partition_broadcast(P)).then_inc(attn1_in, 16)

            @block.vector
            def _(dve):
                def keep(i, b):
                    u = 2 * i + b
                    wait(dve, xT_ready, u + 1)
                    nc.vector.tensor_copy(xn2T[:, :, ds(tile0(i, b) * P, UN)], xTv[:, b, :, :]).then_inc(xT2_ready, 1)
                    wait(dve, lg_ready, u + 1)
                    nc.vector.tensor_copy(lg[:, ds(tile0(i, b), UT), :],
                                          psum[2 + b][:, 0:UT * (E + 1)].rearrange("p (t e) -> p t e", t=UT)).then_inc(lg_taken, 1)

                def unit(i, b, first, last):
                    ln.stats(dve, x, i, b)
                    if not first:
                        keep(i - 1, b)

                over_units(dve, unit)
                keep(NU // 2 - 1, 0)
                keep(NU // 2 - 1, 1)
                dve.wait_ge(lg_taken, NU)

            @block.gpsimd
            def _(pool):
                def keep(i, b):
                    wait(pool, ln.xn_ready, UT * (2 * i + b) + UT)
                    for t in range(UT):
                        nc.gpsimd.tensor_copy(xn2[:, ds(tile0(i, b) + t, 1), :], mem["xn"][:, b, t:t + 1, :]).then_inc(kept, 1)

                def unit(i, b, first, last):
                    ln.rstd(pool, i, b)
                    if not (first and b == 0):
                        keep(*((i, 0) if b else (i - 1, 1)))
                over_units(pool, unit)
                keep(NU // 2 - 1, 1)

            @block.tensor
            def _(pe):
                pe.wait_ge(router_in, 16)

                def route(i, b):
                    u = 2 * i + b
                    wait(pe, xT_ready, u + 1)
                    wait(pe, lg_taken, u - 1)
                    for t in range(UT):
                        for k in range(KD):
                            last = nc.tensor.matmul(psum[2 + b][:, t * (E + 1):(t + 1) * (E + 1)],
                                                    xTv[:, b, k, t * P:(t + 1) * P], gw[:, k, :],
                                                    start=(k == 0), stop=(k == KD - 1))
                    last.then_inc(lg_ready, 1)

                def unit(i, b, first, last_pair):
                    u = 2 * i + b
                    wait(pe, ln.xn_ready, UT * u + UT)
                    wait(pe, xT_ready, u - 1)
                    for t in range(UT):
                        for k in range(KD):
                            last = nc.tensor.transpose(psum[b][:, k * UN + t * P:k * UN + (t + 1) * P],
                                                       mem["xn"][:, b, t, k * P:(k + 1) * P], mem["ident"][:, :])
                    last.then_inc(xt_ready, 1)
                    if not (first and b == 0):
                        route(*((i, 0) if b else (i - 1, 1)))

                over_units(pe, unit)
                route(NU // 2 - 1, 1)

            @block.scalar
            def _(act):
                def copy(i, b):
                    u = 2 * i + b
                    wait(act, xt_ready, u + 1)
                    wait(act, lg_ready, u - 1)
                    wait(act, xT2_ready, u - 1)
                    nc.scalar.activation(xTv[:, b, :, :], psum[b][:, :].rearrange("p (k n) -> p k n", k=KD),
                                         ACT.Copy).then_inc(xT_ready, 1)

                def unit(i, b, first, last):
                    u = 2 * i + b
                    wait(act, kept, UT * (u - 1))
                    wait(act, xt_ready, u - 1)
                    ln.normalise(act, x, i, b)
                    if not (first and b == 0):
                        copy(*((i, 0) if b else (i - 1, 1)))
                over_units(act, unit)
                copy(NU // 2 - 1, 1)

        hot = {n: sb("rt_" + n, [P, NT, E]) for n in ("p", "key", "hot1", "rest", "hot2", "mask", "slots")}
        col = {n: sb("rc_" + n, [P, NT]) for n in ("max", "sum", "inv", "kmax", "sg")}
        wtop = sb("wtop", [P, 2, NT])
        slot_f = sb("slot_f", [P, 2, NT])
        slot = sb("slot", [P, 2, NT], I32)
        rev = sb("rev", [P, E])
        before = sb("before", [P, P])
        ones = sb("ones", [P, P])
        thr = sb("thr", [P, NT])
        blk = sb("blk", [P, NB])
        cnt = sb("cnt", [P, 4, E])
        cmp_n = sb("cmp_n", [P, E, NT])
        cmp_b = sb("cmp_b", [P, NB, E])
        be_f = sb("be_f", [P, NB])
        be = sb("be", [1, NB], I32)
        one8 = sb("one8", [P, E])
        cst, rt, ex_done, masked, ranked, routed, scattered = (
            sem("cst"), sem("rt"), sem("ex_done"), sem("masked"), sem("ranked"), sem("routed"), sem("scattered"))
        g_ready, u_ready, silu_done, h_done, d_ready, sh_added = (
            sem("sh_g_ready"), sem("sh_u_ready"), sem("sh_silu_done"), sem("sh_h_done"), sem("sh_d_ready"), sem("sh_added"))
        act_s = mem["pw"]
        hT = big[:, 0:2 * KS * SG].rearrange("p (b j n) -> p b j n", b=2, j=KS)
        NSG = NT * P // SG
        with nc.Block() as block:
            @block.gpsimd
            def _(pool):
                nc.gpsimd.iota(rev[:, :], [[-1, E]], base=E, channel_multiplier=0, allow_small_or_imprecise_dtypes=True).then_inc(cst, 1)
                nc.gpsimd.iota(thr[:, :], [[P, NT]], base=0, channel_multiplier=0, allow_small_or_imprecise_dtypes=True).then_inc(cst, 1)
                nc.gpsimd.iota(blk[:, :], [[1, NB]], base=0, channel_multiplier=0, allow_small_or_imprecise_dtypes=True).then_inc(cst, 1)
                nc.gpsimd.memset(ones[:, :], 1.0).then_inc(cst, 1)
                nc.gpsimd.memset(before[:, :], 1.0).then_inc(cst, 1)
                nc.gpsimd.memset(one8[:, :], 1.0).then_inc(cst, 1)
                pool.wait_ge(cst, 6)
                nc.gpsimd.affine_select(out=before[:, :], in_=before[:, :], compare_op=ALU.is_ge, fill=0.0,
                                        base=-1, pattern=[[1, P]], channel_multiplier=-1).then_inc(cst, 1)
                pool.wait_ge(routed, 1)
                pool.wait_ge(rows_zeroed, 16)
                for t in range(NT):
                    for j in range(2):
                        pool.indirect_dma_start(xg_dram[:, :], bass.IndirectOffsetOnAxis(ap=slot[:, j, t:t + 1], axis=0),
                                                xn2[:, t, :], None, bounds_check=SLOTS - 1).then_inc(scattered, 16)
                pool.wait_ge(scattered, 16 * 2 * NT)

            @block.scalar
            def _(act):
                act.wait_ge(rt, 2)
                nc.scalar.activation(hot["p"][:, :, :], hot["p"][:, :, :], ACT.Exp).then_inc(ex_done, 1)
                nc.scalar.activation(col["sg"][:, :], lg[:, :, E], ACT.Exp, scale=-1.0).then_inc(ex_done, 1)

                def group(gi, par, first):
                    for j in range(KS):
                        n = KS * (2 * gi + par) + j
                        rows = SR[j]
                        wait(act, g_ready, n + 1)
                        wait(act, h_done, n - 1)
                        nc.scalar.activation(act_s[0:rows, j % 2, :], psum[j % 2][0:rows, :], ACT.Silu).then_inc(silu_done, 1)
                over_pairs(act, NSG // 2, lambda gi: [group(gi, par, False) for par in range(2)])

            @block.tensor
            def _(pe):
                rank = psum[6][:, 0:(NT + 1) * E].rearrange("p (t e) -> p t e", e=E)
                pe.wait_ge(masked, 1)
                pe.wait_ge(cst, 7)
                for t in range(NT):
                    nc.tensor.matmul(rank[:, t + 1:NT + 1, :], ones[:, :],
                                     hot["mask"][:, t:t + 1, :].to_broadcast([P, NT - t, E]),
                                     start=(t == 0), stop=False, skip_group_check=True)
                nc.tensor.matmul(rank[:, 0:1, :], before[:, :], hot["mask"][:, 0:1, :], start=False, stop=False,
                                 skip_group_check=True)
                nc.tensor.matmul(rank[:, 1:NT, :], before[:, :], hot["mask"][:, 1:NT, :], start=False, stop=True,
                                 skip_group_check=True).then_inc(ranked, 1)
                pe.wait_ge(shared_in, 64)

                def up(gi, par):
                    for j in range(KS):
                        n = KS * (2 * gi + par) + j
                        rows = SR[j]
                        wait(pe, silu_done, n - 1)
                        wait(pe, h_done, n - 1)
                        for w, bank, done in ((0, j % 2, g_ready), (1, 2 + j % 2, u_ready)):
                            for k in range(KD):
                                last = nc.tensor.matmul(psum[bank][0:rows, :], sgu[:, w, k, j * P:j * P + rows],
                                                        xn2T[:, k, ds((2 * gi + par) * SG, SG)],
                                                        start=(k == 0), stop=(k == KD - 1))
                            last.then_inc(done, 1)

                def down(gi, par):
                    g = 2 * gi + par
                    wait(pe, h_done, KS * g + KS)
                    for c in range(2):
                        wait(pe, sh_added, 4 * g + 2 * c - 2)
                        for t in range(2):
                            for j in range(KS):
                                last = nc.tensor.matmul(psum[4 + c][:, t * D:(t + 1) * D],
                                                        hT[0:SR[j], par, j, (2 * c + t) * P:(2 * c + t + 1) * P],
                                                        sdn[0:SR[j], j, :], start=(j == 0), stop=(j == KS - 1))
                            last.then_inc(d_ready, 1)

                def pair(gi):
                    up(gi, 0)
                    up(gi, 1)
                    down(gi, 0)
                    down(gi, 1)

                over_pairs(pe, NSG // 2, pair)

            @block.vector
            def _(dve):
                v = nc.vector
                n = 0

                def link(ins):
                    nonlocal n
                    n += 1
                    ins.then_inc(rt, 1)
                    dve.wait_ge(rt, n)

                wide = lambda a: a.unsqueeze(2).to_broadcast([P, NT, E])
                link(v.tensor_reduce(col["max"][:, :], lg[:, :, 0:E], AX.X, ALU.max))
                link(v.tensor_tensor(hot["p"][:, :, :], lg[:, :, 0:E], wide(col["max"][:, :]), ALU.subtract))
                dve.wait_ge(ex_done, 2)
                link(v.tensor_reduce(col["sum"][:, :], hot["p"][:, :, :], AX.X, ALU.add))
                link(v.reciprocal(col["inv"][:, :], col["sum"][:, :]))
                link(v.tensor_tensor(hot["p"][:, :, :], hot["p"][:, :, :], wide(col["inv"][:, :]), ALU.mult))
                link(v.tensor_scalar(col["sg"][:, :], col["sg"][:, :], 1.0, None, ALU.add))
                link(v.reciprocal(col["sg"][:, :], col["sg"][:, :]))
                dve.wait_ge(cst, 7)
                n = top_two(nc, dve, rt, n, hot["p"][:, :, :], rev[:, :].unsqueeze(1).to_broadcast([P, NT, E]),
                            (hot["key"][:, :, :], wtop[:, 0, :], hot["hot1"][:, :, :], hot["rest"][:, :, :],
                             wtop[:, 1, :], hot["hot2"][:, :, :], col["kmax"][:, :]), [P, NT, E], -2.0)
                v.tensor_tensor(hot["mask"][:, :, :], hot["hot1"][:, :, :], hot["hot2"][:, :, :], ALU.add).then_inc(masked, 1)
                dve.wait_ge(ranked, 1)
                rank = psum[6][:, 0:(NT + 1) * E].rearrange("p (t e) -> p t e", e=E)
                link(v.tensor_copy(cnt[:, 0, :], rank[:, NT, :]))
                link(v.tensor_tensor(cmp_n[:, :, :], cnt[:, 0, :].unsqueeze(2).to_broadcast([P, E, NT]),
                                     thr[:, :].unsqueeze(1).to_broadcast([P, E, NT]), ALU.is_gt))
                link(v.tensor_reduce(cnt[:, 1, :], cmp_n[:, :, :], AX.X, ALU.add))
                link(v.tensor_tensor_scan(cnt[:, 2, :], one8[:, :], cnt[:, 1, :], 0.0, ALU.mult, ALU.add))
                link(v.tensor_tensor(cnt[:, 3, :], cnt[:, 2, :], cnt[:, 1, :], ALU.subtract))
                link(v.tensor_scalar(cnt[:, 3, :], cnt[:, 3, :], float(P), None, ALU.mult))
                link(v.tensor_tensor(hot["slots"][:, :, :], rank[:, 0:NT, :],
                                     cnt[:, 3, :].unsqueeze(1).to_broadcast([P, NT, E]), ALU.add))
                for j, h in enumerate(("hot1", "hot2")):
                    link(v.tensor_tensor(hot["key"][:, :, :], hot[h][:, :, :], hot["slots"][:, :, :], ALU.mult))
                    link(v.tensor_reduce(slot_f[:, j, :], hot["key"][:, :, :], AX.X, ALU.add))
                link(v.tensor_tensor(cmp_b[:, :, :], cnt[:, 2, :].unsqueeze(1).to_broadcast([P, NB, E]),
                                     blk[:, :].unsqueeze(2).to_broadcast([P, NB, E]), ALU.is_le))
                link(v.tensor_reduce(be_f[:, :], cmp_b[:, :, :], AX.X, ALU.add))
                link(v.tensor_scalar(be_f[:, :], be_f[:, :], float(E - 1), None, ALU.min))
                link(v.tensor_copy(be[:, :], be_f[0:1, :]))
                v.tensor_copy(slot[:, :, :], slot_f[:, :, :]).then_inc(routed, 1)

                def hidden(gi, par):
                    for j in range(KS):
                        n = KS * (2 * gi + par) + j
                        rows = SR[j]
                        wait(dve, silu_done, n + 1)
                        wait(dve, u_ready, n + 1)
                        wait(dve, d_ready, 4 * (2 * gi + par - 1))
                        v.tensor_tensor(hT[0:rows, par, j, :], psum[2 + j % 2][0:rows, :], act_s[0:rows, j % 2, :],
                                        ALU.mult).then_inc(h_done, 1)

                def add(gi, par):
                    g = 2 * gi + par
                    for t in range(4):
                        wait(dve, d_ready, 4 * g + 2 * (t // 2) + 2)
                        rows = x[:, ds(4 * g + t, 1), :].squeeze(1)
                        v.scalar_tensor_tensor(rows, psum[4 + t // 2][:, (t % 2) * D:(t % 2 + 1) * D],
                                               col["sg"][:, ds(4 * g + t, 1)], rows, ALU.mult, ALU.add).then_inc(sh_added, 1)

                def pair(gi):
                    hidden(gi, 0)
                    hidden(gi, 1)
                    add(gi, 0)
                    add(gi, 1)

                over_pairs(dve, NSG // 2, pair)
                dve.wait_ge(sh_added, NT)

        at, parts = 0, {}
        for name, shape in (("xg", (2, D)), ("xgT", (2, KD * P)), ("hh", (2, I)), ("hg", (2, I)), ("hgT", (2, KI * P)),
                            ("yy", (2, D))):
            parts[name] = big[:, at:at + shape[0] * shape[1]].rearrange("p (c n) -> p c n", c=2)
            at += shape[0] * shape[1]
        xg, hh, hg, yy = parts["xg"], parts["hh"], parts["hg"], parts["yy"]
        xgT = parts["xgT"].rearrange("p c (k n) -> p c k n", k=KD)
        hgT = parts["hgT"].rearrange("p c (k n) -> p c k n", k=KI)
        bx_in, bt_ready, bT_done, bg_ready, bu_ready, bsilu, bh_done, bht_ready, bhT_done, by_ready, by_done, by_out = (
            [sem(f"bx_in{c}") for c in range(2)], sem("bt_ready"), sem("bT_done"), sem("bg_ready"), sem("bu_ready"),
            sem("bsilu"), sem("bh_done"), sem("bht_ready"), sem("bhT_done"), sem("by_ready"), sem("by_done"),
            [sem(f"by_out{c}") for c in range(2)])
        HB = NB // 2
        with nc.Block() as block:
            @block.sync
            def _(sp):
                def fetch(i, c):
                    wait(sp, bt_ready, 2 * i + c - 1)
                    sp.dma_start(xg[:, c, :], xg_dram[ds((2 * i + c) * P, P), :]).then_inc(bx_in[c], 16)

                fetch(0, 0)
                fetch(0, 1)
                with sp.Fori(1, HB) as i:
                    fetch(i, 0)
                    fetch(i, 1)

            @block.gpsimd
            def _(pool):
                with pool.Fori(0, HB) as i:
                    for c in range(2):
                        wait(pool, by_done, 2 * i + c + 1)
                        pool.dma_start(yg_dram[ds((2 * i + c) * P, P), :], yy[:, c, :]).then_inc(by_out[c], 16)
                for c in range(2):
                    pool.wait_ge(by_out[c], 16 * HB)

            @block.tensor
            def _(pe):
                pe.wait_ge(expert_in, 48)

                def transpose_x(i, c):
                    b = 2 * i + c
                    wait(pe, bx_in[c], 16 * i + 16)
                    wait(pe, bT_done, b)
                    for k in range(KD):
                        last = nc.tensor.transpose(psum[0][:, k * P:(k + 1) * P], xg[:, c, k * P:(k + 1) * P], mem["ident"][:, :])
                    last.then_inc(bt_ready, 1)

                def half(i, c, w, bank, done, taken, e):
                    b = 2 * i + c
                    wait(pe, bT_done, b + 1)
                    wait(pe, taken, b - 1)
                    for k in range(KD):
                        last = nc.tensor.matmul(psum[bank + c][:, 0:I], xgT[:, c, k, :], egu[:, k, ds(e * (2 * I) + w * I, I)],
                                                start=(k == 0), stop=(k == KD - 1))
                    last.then_inc(done, 1)

                def transpose_h(i, c):
                    b = 2 * i + c
                    wait(pe, bh_done, b + 1)
                    wait(pe, bhT_done, b)
                    for k in range(KI):
                        last = nc.tensor.transpose(psum[5][0:IR[k], k * P:(k + 1) * P], hh[:, c, k * P:k * P + IR[k]], mem["ident"][:, :])
                    last.then_inc(bht_ready, 1)

                def down(i, c, e):
                    b = 2 * i + c
                    wait(pe, bhT_done, b + 1)
                    wait(pe, by_done, b)
                    for k in range(KI):
                        last = nc.tensor.matmul(psum[6][:, 0:D], hgT[0:IR[k], c, k, :], edn[0:IR[k], k, ds(e * D, D)],
                                                start=(k == 0), stop=(k == KI - 1))
                    last.then_inc(by_ready, 1)

                next_e = [pe.alloc_register(f"next_expert{c}") for c in range(2)]

                def load_experts(i):
                    pe.reg_load(next_e, be[0:1, ds(2 * i, 2)])

                last_e = pe.alloc_register("last_expert")

                def pair(i, first=False, last=False):
                    e0, e1 = [pe.snap(r, min_val=0, max_val=E - 1) for r in next_e]
                    half(i, 0, 0, 1, bg_ready, bsilu, e0)
                    if not first:
                        transpose_h(i - 1, 1)
                    transpose_x(i, 1)
                    half(i, 0, 1, 3, bu_ready, bh_done, e0)
                    if not first:
                        down(i - 1, 1, pe.snap(last_e, min_val=0, max_val=E - 1))
                    half(i, 1, 0, 1, bg_ready, bsilu, e1)
                    if not last:
                        load_experts(i + 1)
                    transpose_h(i, 0)
                    if not last:
                        transpose_x(i + 1, 0)
                    half(i, 1, 1, 3, bu_ready, bh_done, e1)
                    down(i, 0, e0)
                    pe.reg_mov(last_e, e1)

                load_experts(0)
                transpose_x(0, 0)
                pair(0, first=True)
                with pe.Fori(1, HB - 1) as i:
                    pair(i)
                pair(HB - 1, last=True)
                transpose_h(HB - 1, 1)
                down(HB - 1, 1, pe.snap(last_e, min_val=0, max_val=E - 1))

            @block.scalar
            def _(act):
                def copy_x(i, c):
                    b = 2 * i + c
                    wait(act, bt_ready, b + 1)
                    wait(act, bu_ready, b - 1)
                    nc.scalar.activation(xgT[:, c, :, :], psum[0][:, 0:D].rearrange("p (k n) -> p k n", k=KD), ACT.Copy).then_inc(bT_done, 1)

                def silu(i, c):
                    b = 2 * i + c
                    wait(act, bg_ready, b + 1)
                    wait(act, bh_done, b - 1)
                    nc.scalar.activation(hg[:, c, :], psum[1 + c][:, 0:I], ACT.Silu).then_inc(bsilu, 1)

                def copy_h(i, c):
                    b = 2 * i + c
                    wait(act, bht_ready, b + 1)
                    wait(act, by_ready, b - 1)
                    nc.scalar.activation(hgT[:, c, 0:2, :], psum[5][:, 0:2 * P].rearrange("p (k n) -> p k n", k=2), ACT.Copy)
                    nc.scalar.activation(hgT[0:IR[2], c, 2, :], psum[5][0:IR[2], 2 * P:3 * P], ACT.Copy).then_inc(bhT_done, 1)

                def pair(i, first=False, last=False):
                    silu(i, 0)
                    if not first:
                        copy_h(i - 1, 1)
                    copy_x(i, 1)
                    silu(i, 1)
                    copy_h(i, 0)
                    if not last:
                        copy_x(i + 1, 0)

                copy_x(0, 0)
                pair(0, first=True)
                with act.Fori(1, HB - 1) as i:
                    pair(i)
                pair(HB - 1, last=True)
                copy_h(HB - 1, 1)

            @block.vector
            def _(dve):
                def hidden(i, c):
                    b = 2 * i + c
                    wait(dve, bsilu, b + 1)
                    wait(dve, bu_ready, b + 1)
                    wait(dve, bht_ready, b - 1)
                    nc.vector.tensor_tensor(hh[:, c, :], psum[3 + c][:, 0:I], hg[:, c, :], ALU.mult).then_inc(bh_done, 1)

                def take_y(i, c):
                    b = 2 * i + c
                    wait(dve, by_ready, b + 1)
                    if not isinstance(i, int) or i >= 1:
                        wait(dve, by_out[c], 16 * i)
                    nc.vector.tensor_copy(yy[:, c, :], psum[6][:, 0:D]).then_inc(by_done, 1)

                hidden(0, 0)
                hidden(0, 1)
                take_y(0, 0)
                hidden(1, 0)
                take_y(0, 1)
                with dve.Fori(1, HB - 1) as i:
                    hidden(i, 1)
                    take_y(i, 0)
                    hidden(i + 1, 0)
                    take_y(i, 1)
                hidden(HB - 1, 1)
                take_y(HB - 1, 0)
                take_y(HB - 1, 1)

        kv_setup(nc, ctx, "kv1", mem, psum, wk, wv, attn1_in, 16 * 8, bcol[:, 1, :], bvrow, kb, vb)
        attention(nc, ctx, "attn1", mem, psum, x, wq[1], wo[1], kb, vb, bcol[:, 0, :], bo_all, attn1_in, 16 * 8,
                  combine={"w": wtop, "slot": slot, "y": yg_dram})

        fa = big[:, 0:KR * D].rearrange("p (k n) -> p k n", k=KR)
        fb = big[:, KR * D:2 * KR * D].rearrange("p (k n) -> p k n", k=KR)
        fbg = big[:, 2 * KR * D:(2 + B) * KR * D].rearrange("p (b k n) -> p b k n", b=B, k=KR)
        o0 = (2 + B) * KR * D
        wb = big[:, o0:o0 + B * KD * D].rearrange("p (b k n) -> p b k n", b=B, k=KD)
        o1 = o0 + B * KD * D
        xcol = big[:, o1:o1 + B * KD * P].rearrange("p (b k n) -> p b k n", b=B, k=KD)
        o2 = o1 + B * KD * P
        fo = big[:, o2:o2 + 2 * UT * D].rearrange("p (b t n) -> p b t n", b=2, t=UT)
        fs = xn2[:, 0:2 * UT, :].rearrange("p (b t) n -> p b t n", b=2)
        wr = sb("wr", [P, KD, E])
        gt = {n: sb("gt_" + n, [P, B, E]) for n in ("p", "key", "hot1", "rest", "hot2", "gate")}
        gc = {n: sb("gc_" + n, [P, B]) for n in ("top1", "top2", "kmax", "d", "e", "den", "inv")}
        gcol = sb("gcol", [P, B, KR])
        ln3 = LayerNorm(nc, ctx, "ln3", mem)
        f_xt, f_xT, f_col, f_lg, f_g, f_exp, f_gcol, f_scaled, f_w, f_wb, f_y, f_added, f_out, f_sum, f_sum2 = (
            sem(n) for n in ("f_xt", "f_xT", "f_col", "f_lg", "f_g", "f_exp", "f_gcol", "f_scaled", "f_w", "f_wb", "f_y",
                             "f_added", "f_out", "f_sum", "f_sum2"))
        f_store = [sem(f"f_store{b}") for b in range(2)]
        out_t = out.rearrange("(t p) n -> p t n", p=P)
        with nc.Block() as block:
            @block.sync
            def _(sp):
                sp.dma_start(fa, a_in.rearrange("(k p) n -> p k n", p=P)).then_inc(ffn1_in, 16)
                sp.dma_start(fb, bw_in.rearrange("(k p) n -> p k n", p=P)).then_inc(ffn1_in, 16)
                sp.dma_start(wr[:, :, :], split(wr_in)).then_inc(ffn1_in, 16)
                with sp.Fori(0, NU // 2) as i:
                    for b in range(B):
                        wait(sp, f_added, 2 * i + b + 1)
                        sp.dma_start(out_t[:, ds(tile0(i, b), UT), :], fo[:, b, :, :]).then_inc(f_store[b], 16)
                for b in range(B):
                    sp.wait_ge(f_store[b], 16 * NU // 2)

            @block.gpsimd
            def _(pool):
                def add_norm(i, b):
                    wait(pool, ln3.xn_ready, UT * (2 * i + b) + UT)
                    wait(pool, f_added, 2 * i + b - 1)
                    nc.gpsimd.tensor_tensor(fs[:, b, :, :], mem["xn"][:, b, :, :], x[:, ds(tile0(i, b), UT), :],
                                            ALU.add).then_inc(f_sum2, 1)

                def unit(i, b, first, last):
                    ln3.rstd(pool, i, b)
                    if not (first and b == 0):
                        add_norm(*((i, 0) if b else (i - 1, 1)))
                over_units(pool, unit)
                add_norm(NU // 2 - 1, 1)

            @block.tensor
            def _(pe):
                def front(i, b):
                    u = 2 * i + b
                    wait(pe, ln3.xn_ready, UT * u + UT)
                    wait(pe, f_xT, u - 1)
                    for t in range(UT):
                        for k in range(KD):
                            last = nc.tensor.transpose(psum[b][:, k * UN + t * P:k * UN + (t + 1) * P],
                                                       mem["xn"][:, b, t, k * P:(k + 1) * P], mem["ident"][:, :])
                    last.then_inc(f_xt, 1)

                def back(i, b):
                    u = 2 * i + b
                    wait(pe, f_xT, u + 1)
                    wait(pe, f_added, u - 1)
                    for t in range(UT):
                        for k in range(KD):
                            last = nc.tensor.matmul(psum[2 + b][:, t * D:(t + 1) * D], xTv[:, b, k, t * P:(t + 1) * P],
                                                    wb[:, b, k, :], start=(k == 0), stop=(k == KD - 1))
                    last.then_inc(f_y, 1)

                front(0, 0)
                front(0, 1)
                pe.wait_ge(ffn1_in, 48)
                pe.wait_ge(f_col, B * KD)
                for b in range(B):
                    for k in range(KD):
                        last = nc.tensor.matmul(psum[4][:, b * E:(b + 1) * E], xcol[:, b, k, :], wr[:, k, :],
                                                start=(k == 0), stop=(k == KD - 1))
                last.then_inc(f_lg, 1)
                pe.wait_ge(f_scaled, B * KR)
                for b in range(B):
                    for m in range(KD):
                        for k in range(KR):
                            last = nc.tensor.matmul(psum[6 + b][:, m * D:(m + 1) * D], fa[:, k, m * P:(m + 1) * P],
                                                    fbg[:, b, k, :], start=(k == 0), stop=(k == KR - 1))
                last.then_inc(f_w, 1)
                pe.wait_ge(f_wb, B)

                def pair(i):
                    for b in range(B):
                        back(i, b)
                        front(i + 1, b)

                over_pairs(pe, NU // 2 - 1, pair)
                for b in range(B):
                    back(NU // 2 - 1, b)

            @block.scalar
            def _(act):
                def copy(i, b):
                    u = 2 * i + b
                    wait(act, f_xt, u + 1)
                    wait(act, f_y, u - 1)
                    nc.scalar.activation(xTv[:, b, :, :], psum[b][:, :].rearrange("p (k n) -> p k n", k=KD),
                                         ACT.Copy).then_inc(f_xT, 1)

                def normalise(i, b):
                    wait(act, f_xt, 2 * i + b - 1)
                    wait(act, f_sum2, 2 * i + b - 1)
                    ln3.normalise(act, x, i, b)

                for b in range(B):
                    normalise(0, b)
                    copy(0, b)
                for b in range(B):
                    normalise(1, b)
                act.wait_ge(f_g, 1)
                nc.scalar.activation(gc["e"][:, :], gc["d"][:, :], ACT.Exp).then_inc(f_exp, 1)
                act.wait_ge(f_w, 1)
                for b in range(B):
                    nc.scalar.activation(wb[:, b, :, :], psum[6 + b][:, :].rearrange("p (k n) -> p k n", k=KD),
                                         ACT.Copy).then_inc(f_wb, 1)
                with act.Fori(1, NU // 2 - 1) as i:
                    for b in range(B):
                        copy(i, b)
                        normalise(i + 1, b)
                for b in range(B):
                    copy(NU // 2 - 1, b)

            @block.vector
            def _(dve):
                v = nc.vector

                def front(i, b):
                    ln3.stats(dve, x, i, b)

                def back(i, b, later):
                    u = 2 * i + b
                    wait(dve, f_y, u + 1)
                    wait(dve, f_sum2, u + 1)
                    if later:
                        wait(dve, f_store[b], 16 * i)
                    v.tensor_tensor(fo[:, b, :, :], psum[2 + b][:, :].rearrange("p (t n) -> p t n", t=UT),
                                    fs[:, b, :, :], ALU.add).then_inc(f_added, 1)

                front(0, 0)
                front(0, 1)
                dve.wait_ge(f_xT, 2)
                for b in range(B):
                    for k in range(KD):
                        v.tensor_copy(xcol[:, b, k, :], xTv[:, b, k, 0:1].to_broadcast([P, P])).then_inc(f_col, 1)
                for b in range(B):
                    front(1, b)
                dve.wait_ge(f_lg, 1)
                n = 0

                def link(ins):
                    nonlocal n
                    n += 1
                    ins.then_inc(f_sum, 1)
                    dve.wait_ge(f_sum, n)

                link(v.tensor_copy(gt["p"][:, :, :], psum[4][:, 0:B * E].rearrange("p (b e) -> p b e", b=B)))
                n = top_two(nc, dve, f_sum, n, gt["p"][:, :, :], rev[:, :].unsqueeze(1).to_broadcast([P, B, E]),
                            (gt["key"][:, :, :], gc["top1"][:, :], gt["hot1"][:, :, :], gt["rest"][:, :, :],
                             gc["top2"][:, :], gt["hot2"][:, :, :], gc["kmax"][:, :]), [P, B, E], -1e30)
                v.tensor_tensor(gc["d"][:, :], gc["top2"][:, :], gc["top1"][:, :], ALU.subtract).then_inc(f_g, 1)
                dve.wait_ge(f_exp, 1)
                link(v.tensor_scalar(gc["den"][:, :], gc["e"][:, :], 1.0, None, ALU.add))
                link(v.reciprocal(gc["inv"][:, :], gc["den"][:, :]))
                wide = lambda a: a.unsqueeze(2).to_broadcast([P, B, E])
                link(v.tensor_tensor(gt["gate"][:, :, :], gt["hot2"][:, :, :], wide(gc["e"][:, :]), ALU.mult))
                link(v.tensor_tensor(gt["gate"][:, :, :], gt["gate"][:, :, :], gt["hot1"][:, :, :], ALU.add))
                link(v.tensor_tensor(gt["gate"][:, :, :], gt["gate"][:, :, :], wide(gc["inv"][:, :]), ALU.mult))
                for b in range(B):
                    pairs = gt["gate"][:, b, :].rearrange("p (k q) -> p k q", q=2)
                    for q in range(2):
                        v.tensor_copy(gcol[q * R:(q + 1) * R, b, :], pairs[q * R:(q + 1) * R, :, q]).then_inc(f_gcol, 1)
                dve.wait_ge(f_gcol, 2 * B)
                dve.wait_ge(ffn1_in, 48)
                for b in range(B):
                    for k in range(KR):
                        v.tensor_scalar(fbg[:, b, k, :], fb[:, k, :], gcol[:, b, k:k + 1], None, ALU.mult).then_inc(f_scaled, 1)
                for b in range(B):
                    front(2, b)
                    back(0, b, False)
                with dve.Fori(1, NU // 2 - 2) as i:
                    for b in range(B):
                        front(i + 2, b)
                        back(i, b, True)
                for i in (NU // 2 - 2, NU // 2 - 1):
                    for b in range(B):
                        back(i, b, True)
                dve.wait_ge(f_added, NU)


def kernel(**inputs):
    import numpy as np
    import concourse.bacc as bacc
    from concourse import mybir as mb
    from concourse.bass_utils import run_bass_kernel_spmd as run

    g = {k: np.asarray(v) for k, v in inputs.items()}
    nb, ns, nd = g["x"].shape
    ne, ni2 = g["L0_ffn_experts_gate_up"].shape[:2]
    ni = g["L0_ffn_experts_down"].shape[2]
    nr = g["L1_ffn_A"].shape[1]
    laid = [
        ("x", g["x"].reshape(nb * ns, nd)),
        ("ctxT", g["ctx_1024"].reshape(-1, nd).T),
        ("wq0", g["L0_xattn_W_q"].T), ("wk0", g["L0_xattn_W_k"].T), ("wv0", g["L0_xattn_W_v"].T), ("wo0", g["L0_xattn_W_fc"].T),
        ("gate", np.concatenate([g["L0_ffn_gate_w"], g["L0_ffn_shared_expert_gate_w"]], axis=0).T),
        ("egu", g["L0_ffn_experts_gate_up"].transpose(2, 0, 1).reshape(nd, ne * ni2)),
        ("edown", g["L0_ffn_experts_down"].transpose(2, 0, 1).reshape(ni, ne * nd)),
        ("sgate", g["L0_ffn_shared_gate_w"].T), ("sup", g["L0_ffn_shared_up_w"].T), ("sdown", g["L0_ffn_shared_down_w"].T),
        ("wq1", g["L1_xattn_Wq"]), ("bq1", g["L1_xattn_bq"]), ("wk1", g["L1_xattn_Wk"]), ("bk1", g["L1_xattn_bk"]),
        ("wv1", g["L1_xattn_Wv"]), ("bv1", g["L1_xattn_bv"]), ("wo1", g["L1_xattn_Wo"]), ("bo1", g["L1_xattn_bo"]),
        ("wr", g["L1_ffn_Wr"].T), ("a", g["L1_ffn_A"].reshape(ne * nr, nd)),
        ("bw", g["L1_ffn_Bw"].transpose(0, 2, 1).reshape(ne * nr, nd)),
    ]
    nc = bacc.Bacc("TRN2", target_bir_lowering=False, num_devices=1)
    arrays, args = {}, []
    for name, a in laid:
        a = np.ascontiguousarray(a)
        arrays[f"in_{name}"] = a
        args.append(nc.dram_tensor(f"in_{name}", a.shape, mb.dt.from_np(a.dtype), kind="ExternalInput").ap())
    out = nc.dram_tensor("out_x", (nb * ns, nd), mb.dt.float32, kind="ExternalOutput").ap()
    xattn_ffn_kernel(nc, *args, out)
    r = run(nc, [arrays], core_ids=[0])
    return r.results[0]["out_x"].reshape(nb, ns, nd)
```
